# Optimizing a Trainium2 kernel written in Bass

```python
import numpy as np
import jax
import jax.numpy as jnp

def _softmax(x, axis=-1):
    return jax.nn.softmax(x, axis=axis)

def _gelu(x):
    return jax.nn.gelu(x, approximate=True)

def _silu(x):
    return jax.nn.silu(x)

def _sigmoid(x):
    return jax.nn.sigmoid(x)

def _layernorm(x, axis=-1, eps=1e-05):
    m = jnp.mean(x, axis=axis, keepdims=True)
    v = jnp.var(x, axis=axis, keepdims=True)
    return (x - m) / jnp.sqrt(v + eps)

def _scatter_add(tgt, idx, src, axis=0):
    return tgt.at[idx].add(src)

def _segment_sum(src, seg, n):
    return jax.ops.segment_sum(src, seg, n)
kernel_name = 'mk_xattn_ffn_d1_seqx_r2_162528'

def setup_inputs(seed: int=0):
    np.random.seed(seed)
    _w = jnp.asarray

    def _rec_inputs():
        import jax
        import jax.numpy as jnp
        _rk = jax.random.key(seed)
        x = -0.000125 + 0.9999 * jax.random.normal(jax.random.fold_in(_rk, 1), (8, 224, 1024), jnp.float32)
        _lenS = 224 - jax.random.randint(jax.random.fold_in(_rk, 7), (8,), 0, max(1, 224 // 4) + 1, jnp.int32)
        _lenS2 = 750 - jax.random.randint(jax.random.fold_in(_rk, 8), (8,), 0, max(1, 750 // 4) + 1, jnp.int32)
        _ctx_2048P = jax.random.normal(jax.random.fold_in(_rk, 11), (8, 16, 1024), jnp.float32)
        _ctx_2048c = jax.random.dirichlet(jax.random.fold_in(_rk, 511), 0.3 * jnp.ones((16,), jnp.float32), (8, 750))
        _ctx_2048t = jnp.einsum('bsk,bkd->bsd', _ctx_2048c, _ctx_2048P)
        _ctx_2048t = _ctx_2048t * jax.lax.rsqrt(jnp.mean(jnp.square(_ctx_2048t)) + 1e-12) * 0.953939
        ctx_2048 = -0.000514642 + 1.00011 * (_ctx_2048t + 0.3 * jax.random.normal(jax.random.fold_in(_rk, 611), (8, 750, 1024), jnp.float32))
        _validS = jnp.arange(224)[None, :] < _lenS[:, None]
        _validS2 = jnp.arange(750)[None, :] < _lenS2[:, None]
        _causal = jnp.tril(jnp.ones((224, 224), dtype=bool))
        mask_BxS2_bk0 = jnp.logical_not(jnp.broadcast_to(_validS2[:, :], (8, 750)))
        return (x, ctx_2048, mask_BxS2_bk0)
    x, ctx_2048, mask_BxS2_bk0 = _rec_inputs()

    def _L0_xattn_setup():
        import jax, jax.numpy as jnp
        import numpy as np
        key = jax.random.key(seed)
        k1, k2, k3 = jax.random.split(key, 3)
        B, S, D, M = (8, 1024, 1024, 128)
        hidden_states = jax.random.normal(k1, (B, S, D), dtype=jnp.float32)
        memory_tokens = jax.random.normal(k2, (B, M, D), dtype=jnp.float32)
        memory_mask = jax.random.randint(k3, (B, M), 0, 2).astype(jnp.bool_)
        return {'hidden_states': hidden_states, 'memory_tokens': memory_tokens, 'memory_mask': memory_mask}
    _L0_xattn_all = _L0_xattn_setup()
    _L0_xattn_in = {k: v for k, v in _L0_xattn_all.items() if k in ()}
    del _L0_xattn_all

    def _L0_ffn_setup():
        import jax, jax.numpy as jnp
        import numpy as np
        B_, S, D = (2, 1024, 1024)
        F_ = 4096
        R = 16
        H = 16
        HD = D // H
        MOD_SCALE = 0.1
        EPS = 1e-06

        def _rmsnorm(x, w):
            v = jnp.mean(x * x, axis=-1, keepdims=True)
            return x * jax.lax.rsqrt(v + EPS) * w

        def _attention(x, Wq, Wk, Wv, Wo):
            b, s, d = x.shape
            q = (x @ Wq.T).reshape(b, s, H, HD)
            k = (x @ Wk.T).reshape(b, s, H, HD)
            v = (x @ Wv.T).reshape(b, s, H, HD)
            scores = jnp.einsum('bqhd,bkhd->bhqk', q, k) / np.sqrt(HD).astype(np.float32)
            causal = jnp.tril(jnp.ones((s, s), bool))
            scores = jnp.where(causal, scores, jnp.finfo(scores.dtype).min)
            probs = jax.nn.softmax(scores, axis=-1)
            out = jnp.einsum('bhqk,bkhd->bqhd', probs, v).reshape(b, s, d)
            return out @ Wo.T
        key = jax.random.key(seed)
        ks = jax.random.split(key, 12)
        sd = 0.02
        return {'hidden_states': jax.random.normal(ks[0], (B_, S, D), jnp.float32), 'ln1_w': jnp.ones((D,), jnp.float32), 'ln2_w': jnp.ones((D,), jnp.float32), 'Wq': jax.random.normal(ks[1], (D, D), jnp.float32) * sd, 'Wk': jax.random.normal(ks[2], (D, D), jnp.float32) * sd, 'Wv': jax.random.normal(ks[3], (D, D), jnp.float32) * sd, 'Wo': jax.random.normal(ks[4], (D, D), jnp.float32) * sd, 'A': jax.random.normal(ks[5], (D, R), jnp.float32) * (0.01 / np.sqrt(D)), 'B': jax.random.normal(ks[6], (R, F_), jnp.float32) * (0.01 / np.sqrt(R)), 'W_in_base': jax.random.normal(ks[7], (F_, D), jnp.float32) * sd, 'W_up_base': jax.random.normal(ks[8], (F_, D), jnp.float32) * sd, 'W_down': jax.random.normal(ks[9], (D, F_), jnp.float32) * sd}
    _L0_ffn_all = _L0_ffn_setup()
    _L0_ffn_in = {k: v for k, v in _L0_ffn_all.items() if k in ('ln1_w', 'ln2_w', 'Wq', 'Wk', 'Wv', 'Wo', 'A', 'B', 'W_in_base', 'W_up_base', 'W_down')}
    del _L0_ffn_all
    return {'x': x, 'ctx_2048': ctx_2048, 'mask_BxS2_bk0': mask_BxS2_bk0, 'L0_ffn_ln1_w': _L0_ffn_in['ln1_w'], 'L0_ffn_ln2_w': _L0_ffn_in['ln2_w'], 'L0_ffn_Wq': _L0_ffn_in['Wq'], 'L0_ffn_Wk': _L0_ffn_in['Wk'], 'L0_ffn_Wv': _L0_ffn_in['Wv'], 'L0_ffn_Wo': _L0_ffn_in['Wo'], 'L0_ffn_A': _L0_ffn_in['A'], 'L0_ffn_B': _L0_ffn_in['B'], 'L0_ffn_W_in_base': _L0_ffn_in['W_in_base'], 'L0_ffn_W_up_base': _L0_ffn_in['W_up_base'], 'L0_ffn_W_down': _L0_ffn_in['W_down']}

def reference(x, ctx_2048, mask_BxS2_bk0, L0_ffn_ln1_w, L0_ffn_ln2_w, L0_ffn_Wq, L0_ffn_Wk, L0_ffn_Wv, L0_ffn_Wo, L0_ffn_A, L0_ffn_B, L0_ffn_W_in_base, L0_ffn_W_up_base, L0_ffn_W_down):
    import jax
    import jax.numpy as jnp

    def _L0_xattn_ref(hidden_states, memory_tokens, memory_mask):
        import jax, jax.numpy as jnp
        import numpy as np
        B, S, D = hidden_states.shape
        scale = 1.0 / jnp.sqrt(jnp.asarray(D, hidden_states.dtype))
        scores = jnp.einsum('bsd,bmd->bsm', hidden_states, memory_tokens) * scale
        neg_inf = jnp.asarray(-1e+30, scores.dtype)
        scores = jnp.where(memory_mask[:, None, :], scores, neg_inf)
        attn = jax.nn.softmax(scores, axis=-1)
        readout = jnp.einsum('bsm,bmd->bsd', attn, memory_tokens)
        valid_b = jnp.any(memory_mask, axis=-1)
        out = jnp.where(valid_b[:, None, None], readout, jnp.zeros_like(readout))
        return out

    def _L0_ffn_ref(hidden_states, ln1_w, ln2_w, Wq, Wk, Wv, Wo, A, B, W_in_base, W_up_base, W_down):
        import jax, jax.numpy as jnp
        import numpy as np
        B_, S, D = (2, 1024, 1024)
        F_ = 4096
        R = 16
        H = 16
        HD = D // H
        MOD_SCALE = 0.1
        EPS = 1e-06

        def _rmsnorm(x, w):
            v = jnp.mean(x * x, axis=-1, keepdims=True)
            return x * jax.lax.rsqrt(v + EPS) * w

        def _attention(x, Wq, Wk, Wv, Wo):
            b, s, d = x.shape
            q = (x @ Wq.T).reshape(b, s, H, HD)
            k = (x @ Wk.T).reshape(b, s, H, HD)
            v = (x @ Wv.T).reshape(b, s, H, HD)
            scores = jnp.einsum('bqhd,bkhd->bhqk', q, k) / np.sqrt(HD).astype(np.float32)
            causal = jnp.tril(jnp.ones((s, s), bool))
            scores = jnp.where(causal, scores, jnp.finfo(scores.dtype).min)
            probs = jax.nn.softmax(scores, axis=-1)
            out = jnp.einsum('bhqk,bkhd->bqhd', probs, v).reshape(b, s, d)
            return out @ Wo.T
        residual = hidden_states
        x = _rmsnorm(hidden_states, ln1_w)
        attn = _attention(x, Wq, Wk, Wv, Wo)
        mod = MOD_SCALE * jnp.tanh(attn @ A)
        h = _rmsnorm(residual, ln2_w)
        gate_pre = h @ W_in_base.T + mod * (h @ A) @ B
        gate = jax.nn.silu(gate_pre)
        up = h @ W_up_base.T
        mlp_out = gate * up @ W_down.T
        return residual + mlp_out
    x = x + _L0_xattn_ref(_layernorm(x, axis=-1), ctx_2048, mask_BxS2_bk0)
    x = x + _L0_ffn_ref(_layernorm(x, axis=-1), L0_ffn_ln1_w, L0_ffn_ln2_w, L0_ffn_Wq, L0_ffn_Wk, L0_ffn_Wv, L0_ffn_Wo, L0_ffn_A, L0_ffn_B, L0_ffn_W_in_base, L0_ffn_W_up_base, L0_ffn_W_down)
    return x

_drawn_inputs = setup_inputs


def setup_inputs(seed=0):
    import zlib

    import numpy as np

    out = dict(_drawn_inputs(seed))
    spreads = {'L0_ffn_ln1_w': (1.0, 0.6), 'L0_ffn_ln2_w': (1.0, 0.2)}
    factors = {'L0_ffn_Wq': 200.0,
     'L0_ffn_Wk': 200.0,
     'L0_ffn_Wv': 200.0,
     'L0_ffn_Wo': 200.0,
     'L0_ffn_A': 200.0,
     'L0_ffn_B': 200.0}
    for name, (base, spread) in spreads.items():
        noise = np.random.default_rng([zlib.crc32(name.encode()), seed]).standard_normal(out[name].shape)
        drawn = base * np.exp(spread * noise) if base else spread * noise
        out[name] = jnp.asarray(drawn.astype(out[name].dtype))
    for name, factor in factors.items():
        out[name] = (out[name] * factor).astype(out[name].dtype)
    return out
```

```python
from contextlib import ExitStack

import concourse.bass as bass
from concourse import mybir
from concourse.alu_op_type import AluOpType as ALU

F32 = mybir.dt.float32
F32R = mybir.dt.float32r
U8 = mybir.dt.uint8
ACT = mybir.ActivationFunctionType
AX = mybir.AxisListType

B, S, D, M = 8, 224, 1024, 750
FF, R, H, HD = 4096, 16, 16, 64
P = 128
T = B * S
TS = 112
NT = T // TS
DC = D // P
MC, MS = 6, M // 6
MH = -(-M // 4) * 2
MP = 2 * MH
HP = H // 2
NB = 4
BT = NT // NB
BW = T // NB
VW = H * R + R
NF = FF // P
LN_EPS, RMS_EPS = 1e-5, 1e-6
MOD_SCALE = 0.1
CROSS_SCALE = 1.0 / 32.0
SELF_SCALE = 1.0 / 8.0
MASKED = 1e30
FAR = 3.0e38
PASSES = ((0, 0), (0, 1), (1, 0))


def wait(eng, sem, n):
    if isinstance(n, int) and n <= 0:
        return
    eng.wait_ge(sem, n)


def wait_alone(eng, sem, n, passed):
    wait(eng, sem, n)
    if not isinstance(n, int):
        eng.sem_inc(passed, 1)


class Tile:

    def __init__(self, b, j):
        self.batch = b + j // 2 if j // 2 else b
        self.par = j % 2

    def count(self, per=1, extra=0):
        return self.batch * (2 * per) + (self.par * per + per - extra)

    @property
    def index(self):
        return self.batch * 2 + self.par


def fold(nc, dram, keep):
    ctx = ExitStack()
    with ctx:
        sb = lambda n, s, d=F32: ctx.enter_context(nc.sbuf_tensor(n, s, d))
        sem = lambda n: ctx.enter_context(nc.semaphore(n))
        wo = sb("wo", [P, DC, D])
        wv = sb("wv", [P, HP, D])
        a_sb = sb("a_sb", [P, DC, R])
        woa = sb("woa", [P, HP, 2 * R])
        wvx = sb("wvx", [P, DC, VW])
        b_raw = sb("b_raw", [96, FF])
        b_hi = sb("b_hi", [48, FF], F32R)
        b_stack = sb("b_stack", [96, FF], F32R)
        mask8 = sb("mask8", [TS, B, M], U8)
        xs = sb("xs", [TS, 2, D])
        stats = sb("stats", [TS, 2, 6])
        var = sb("var", [TS, NT])
        ps_woa = ctx.enter_context(nc.psum_tensor("ps_woa", [P, DC, R], F32))
        ps_wv = ctx.enter_context(nc.psum_tensor("ps_wv", [P, 2, 512], F32))
        ident_zero, ident_ready = sem("ident_zero"), sem("ident_ready")
        wo_in, wv_in, small_in, b_in, mask_in = (sem(n) for n in ("wo_in", "wv_in", "small_in", "b_in", "mask_in0"))
        x_in = [sem("x_in0"), sem("x_in1")]
        woa_zero, woa_done, woa_ready, wv_done, wv_evac, wvx_full, wvx_hi = (
            sem(n) for n in ("woa_zero", "woa_done", "woa_ready", "wv_done", "wv_evac", "wvx_full", "wvx_hi"))
        b_zero, b_his, b_split, b_out = sem("b_zero"), sem("b_his"), sem("b_split"), sem("b_out")
        x_stats, x_mv, x_var, x_std, x_rstd, fold_done = (sem(n) for n in ("x_stats", "x_mv", "x_var", "x_std", "x_rstd", "fold_done"))
        passed = {n: sem("passed_" + n) for n in ("sp", "pool", "dve")}
        block = ctx.enter_context(nc.Block())

        @block.sync
        def _(sp):
            for c in range(DC):
                sp.dma_start(wo[:, c, :], dram["wo"][c * P:(c + 1) * P, :]).then_inc(wo_in, 16)
            sp.dma_start(a_sb[:], dram["a"].rearrange("(c p) r -> p c r", p=P)).then_inc(small_in, 16)
            sp.dma_start(keep["ln1"][:], dram["ln1"]).then_inc(small_in, 16)
            sp.dma_start(keep["ln2"][:], dram["ln2"]).then_inc(small_in, 16)
            for t in range(2):
                sp.dma_start(xs[:, t, :], dram["x"][t * TS:(t + 1) * TS, :]).then_inc(x_in[t], 16)
            for hp in range(HP):
                sp.dma_start(wv[:, hp, :], dram["wv"][hp * P:(hp + 1) * P, :]).then_inc(wv_in, 16)
            sp.dma_start(mask8[:], dram["mask"].rearrange("(o b) m -> o b m", o=1).to_broadcast([TS, B, M])).then_inc(mask_in, 16)
            for i in range(3):
                sp.dma_start(b_raw[32 * i:32 * i + R, :], dram["b"]).then_inc(b_in, 16)
            for t in range(2, NT):
                wait(sp, x_mv, t - 1)
                sp.dma_start(xs[:, t % 2, :], dram["x"][t * TS:(t + 1) * TS, :]).then_inc(x_in[t % 2], 16)
            wait(sp, b_split, 3)
            sp.dma_start(dram["b_stack"].rearrange("f k n -> k f n"),
                         b_stack[:].bitcast(F32).rearrange("k (f n) -> k f n", n=P)).then_inc(b_out, 16)
            sp.wait_ge(b_out, 16)

        @block.gpsimd
        def _(pool):
            nc.gpsimd.memset(keep["ident"][:], 0.0).then_inc(ident_zero, 1)
            pool.wait_ge(ident_zero, 1)
            nc.gpsimd.affine_select(out=keep["ident"][:], in_=keep["ident"][:], compare_op=ALU.not_equal, fill=1.0,
                                    base=0, pattern=[[-1, P]], channel_multiplier=1).then_inc(ident_ready, 1)
            nc.gpsimd.memset(keep["causal"][:], 0.0).then_inc(ident_zero, 1)
            pool.wait_ge(ident_zero, 2)
            nc.gpsimd.affine_select(out=keep["causal"][:, TS:2 * TS], in_=keep["causal"][:, TS:2 * TS],
                                    compare_op=ALU.is_ge, fill=-FAR, base=0, pattern=[[-1, TS]],
                                    channel_multiplier=1).then_inc(ident_ready, 1)
            nc.gpsimd.memset(woa[:], 0.0).then_inc(woa_zero, 1)
            nc.gpsimd.memset(b_stack[:].bitcast(F32), 0.0).then_inc(b_zero, 1)

        @block.tensor
        def _(pe):
            pe.wait_ge(small_in, 48)
            pe.wait_ge(wo_in, 16 * DC)
            for ci in range(DC):
                for co in range(DC):
                    last = nc.tensor.matmul(ps_woa[:, ci, :], wo[:, co, ci * P:(ci + 1) * P], a_sb[:, co, :],
                                            start=(co == 0), stop=(co == DC - 1))
            last.then_inc(woa_done, 1)
            pe.wait_ge(woa_ready, 2)
            pe.wait_ge(wv_in, 16 * HP)
            for c in range(DC):
                wait(pe, wv_evac, c - 1)
                for hp in range(HP):
                    last = nc.tensor.matmul(ps_wv[:, c % 2, hp * 2 * R:(hp + 1) * 2 * R],
                                            wv[:, hp, c * P:(c + 1) * P], woa[:, hp, :], start=True, stop=True)
                last.then_inc(wv_done, 1)

        @block.scalar
        def _(act):
            act.wait_ge(woa_zero, 1)
            act.wait_ge(woa_done, 1)
            nc.scalar.activation(woa[0:HD, :, 0:R], ps_woa[0:HD, :, :], ACT.Copy).then_inc(woa_ready, 1)
            nc.scalar.activation(woa[HD:P, :, R:2 * R], ps_woa[HD:P, :, :], ACT.Copy).then_inc(woa_ready, 1)
            act.wait_ge(small_in, 48)
            for c in range(DC):
                act.wait_ge(wv_done, c + 1)
                nc.scalar.activation(wvx[:, c, 0:H * R], ps_wv[:, c % 2, 0:H * R], ACT.Copy,
                                     scale=keep["ln1"][:, c:c + 1]).then_inc(wv_evac, 1)
                nc.scalar.activation(wvx[:, c, H * R:VW], a_sb[:, c, :], ACT.Copy,
                                     scale=keep["ln2"][:, c:c + 1]).then_inc(wvx_full, 1)
            act.wait_ge(wv_evac, DC)
            act.wait_ge(wvx_full, DC)
            nc.scalar.activation(keep["wvx"][:, 0], wvx[:], ACT.Copy).then_inc(wvx_hi, 1)
            act.wait_ge(x_var, 1)
            nc.scalar.activation(var[:], var[:], ACT.Sqrt).then_inc(x_std, 1)

        @block.vector
        def _(dve):
            dve.wait_ge(b_zero, 1)
            dve.wait_ge(b_in, 48)
            nc.vector.tensor_copy(b_stack[0:R, :], b_raw[0:R, :]).then_inc(b_split, 1)
            nc.vector.tensor_copy(b_hi[32:32 + R, :], b_raw[32:32 + R, :]).then_inc(b_his, 1)
            nc.vector.tensor_copy(b_stack[64:64 + R, :], b_raw[64:64 + R, :]).then_inc(b_split, 1)
            dve.wait_ge(b_his, 1)
            nc.vector.tensor_sub(b_stack[32:32 + R, :], b_raw[32:32 + R, :],
                                 b_hi[32:32 + R, :].bitcast(F32)).then_inc(b_split, 1)
            for t in range(NT):
                dve.wait_ge(x_in[t % 2], 16 * (t // 2 + 1))
                wait(dve, x_mv, t)
                for i in range(2):
                    nc.vector.bn_stats(stats[:, i, :], xs[:, t % 2, i * 512:(i + 1) * 512]).then_inc(x_stats, 1)
                dve.wait_ge(x_stats, 2 * t + 2)
                nc.vector.bn_aggr(keep["x_mv"][:, t, :], stats[:]).then_inc(x_mv, 1)
            dve.wait_ge(x_mv, NT)
            nc.vector.tensor_scalar(var[:], keep["x_mv"][:, :, 1], LN_EPS, None, ALU.add).then_inc(x_var, 1)
            dve.wait_ge(mask_in, 16)
            nc.vector.tensor_reduce(keep["valid"][:], mask8[:], AX.X, ALU.max).then_inc(fold_done, 1)
            dve.wait_ge(x_std, 1)
            nc.vector.reciprocal(keep["x_rstd"][:], var[:]).then_inc(x_rstd, 1)
            dve.wait_ge(wvx_hi, 1)
            nc.vector.tensor_sub(keep["wvx"][:, 1], wvx[:], keep["wvx"][:, 0].bitcast(F32)).then_inc(fold_done, 1)


def cross(nc, dram, keep):
    ctx = ExitStack()
    with ctx:
        sb = lambda n, s, d=F32: ctx.enter_context(nc.sbuf_tensor(n, s, d))
        pb = lambda n, s: ctx.enter_context(nc.psum_tensor(n, s, F32))
        sem = lambda n: ctx.enter_context(nc.semaphore(n))
        CTR, CXR = 4, 2
        ctT_raw = sb("ctT_raw", [P, CTR, M])
        ctT = sb("ctT", [P, DC, 2, MP], F32R)
        ctx_raw = sb("ctx_raw", [MS, CXR, D])
        cx = sb("cx", [MS, MC, 2, D], F32R)
        xa = sb("xa", [TS, 2, D])
        xb = sb("xb", [TS, 2, D])
        xn = sb("xn", [TS, D])
        xnT = sb("xnT", [P, 2, DC, TS], F32R)
        prob = sb("prob", [TS, 2, MP])
        pT = sb("pT", [MS, 2, MC, TS], F32R)
        z = sb("z", [TS, D])
        resid = sb("resid", [TS, D])
        zT = sb("zT", [P, 2, DC, TS], F32R)
        bias = sb("bias", [TS, MP])
        mask8 = sb("mask8b", [TS, M], U8)
        vout = sb("vout", [TS, H, 2, R], F32R)
        vlow = sb("vlow", [TS, R])
        low = sb("low", [TS, 2])
        total = sb("total", [TS, 2])
        rinv = sb("rinv", [TS, 1])
        gain = sb("gain", [TS, 1])
        stats = sb("stats2", [TS, 2, 6])
        mv = sb("mv", [TS, 2])
        ve = sb("ve", [TS, 2])
        std = sb("std", [TS, 2])
        rstd = sb("rstd", [TS, 2])
        res_scale, res_bias = sb("res_scale", [TS, 1]), sb("res_bias", [TS, 1])
        ps_s = pb("ps_s", [P, 2, 512])
        ps_r = pb("ps_r", [P, 2, 512])
        ps_t = [pb("ps_t0", [P, 2, 512]), pb("ps_t1", [P, 2, 512])]

        ctT_in = [sem(f"ctT_in{i}") for i in range(CTR)]
        cx_in = [sem(f"cx_in{i}") for i in range(CXR)]
        xa_in, xb_in = [sem("xa_in0"), sem("xa_in1")], [sem("xb_in0"), sem("xb_in1")]
        mask_in, pad_ready, bias_pad = sem("mask_in"), sem("pad_ready"), sem("bias_pad")
        ctT_hi, ctT_lo, ctT_used, cx_hi, cx_lo, cx_used = (sem(n) for n in ("ctT_hi", "ctT_lo", "ctT_used", "cx_hi", "cx_lo", "cx_used"))
        xn_ready, xT_done, xnT_hi, xnT_lo = (sem(n) for n in ("xn_ready", "xT_done", "xnT_hi", "xnT_lo"))
        bias_ready, low_ready, exp_done, pT_done, pT_hi, pT_lo = (sem(n) for n in ("bias_ready", "low_ready", "exp_done", "pT_done", "pT_hi", "pT_lo"))
        rinv_ready, gain_ready, x1_ready, st_ready, mv_ready, ve_half, ve_ready, std_ready, rstd_ready = (
            sem(n) for n in ("rinv_ready", "gain_ready", "x1_ready", "st_ready", "mv_ready", "ve_half", "ve_ready", "std_ready", "rstd_ready"))
        z_ready, rsb_ready, resid_ready, resid_out = (sem(n) for n in ("z_ready", "rsb_ready", "resid_ready", "resid_out"))
        zT_done, zT_hi, zT_lo, zT_out, v_done, v_hi, v_lo, v_out, ha_ready = (
            sem(n) for n in ("zT_done", "zT_hi", "zT_lo", "zT_out", "v_done", "v_hi", "v_lo", "v_out", "ha_ready"))
        passed = {n: sem("passed_" + n) for n in ("sp", "pool", "dve")}
        block = ctx.enter_context(nc.Block())

        def schedule(eng, step):
            def run(b, j, steady):
                def at(k):
                    return Tile(b, j + k) if steady or 0 <= 2 * b + j + k < NT else None
                step(at)
            for t in range(-1, 4):
                run(t // 2, t % 2, False)
            with eng.Fori(2, B - 1) as b:
                run(b, 0, True)
                run(b, 1, True)
            for t in range(NT - 2, NT + 2):
                run(t // 2, t % 2, False)

        @block.sync
        def _(sp):
            def load_ctT(b):
                for c in range(DC):
                    wait_alone(sp, ctT_lo, b * DC + (c - CTR + 1), passed["sp"])
                    sp.dma_start(ctT_raw[:, c % CTR, :], dram["ctxT"][bass.ds(b, 1), c].rearrange("o p m -> p (o m)")).then_inc(ctT_in[c % CTR], 16)

            def load_cx(b):
                for m in range(MC):
                    wait_alone(sp, cx_lo, b * MC + (m - CXR + 1), passed["sp"])
                    sp.dma_start(ctx_raw[:, m % CXR, :], dram["ctx"][bass.ds(b, 1), m].rearrange("o p d -> p (o d)")).then_inc(cx_in[m % CXR], 16)

            def load_xa(t):
                wait_alone(sp, xn_ready, t.count() - 2, passed["sp"])
                sp.dma_start(xa[:, t.par, :], dram["x"][bass.ds(t.index * TS, TS), :]).then_inc(xa_in[t.par], 16)

            def load_xb(t):
                wait(sp, resid_ready, t.count() - 2)
                wait_alone(sp, z_ready, t.count() - 2, passed["sp"])
                sp.dma_start(xb[:, t.par, :], dram["x"][bass.ds(t.index * TS, TS), :]).then_inc(xb_in[t.par], 16)

            def load_mask(b):
                wait_alone(sp, bias_ready, b, passed["sp"])
                sp.dma_start(mask8[:], dram["mask"][bass.ds(b, 1), :].to_broadcast([TS, M])).then_inc(mask_in, 16)

            def batch(b, last):
                if not last:
                    load_xa(Tile(b, 2))
                load_cx(b)
                load_xb(Tile(b, 0))
                if not last:
                    load_mask(b + 1)
                    load_xa(Tile(b, 3))
                    load_ctT(b + 1)
                load_xb(Tile(b, 1))

            load_xa(Tile(0, 0))
            load_xa(Tile(0, 1))
            load_mask(0)
            load_ctT(0)
            batch(0, False)
            with sp.Fori(1, B - 1) as b:
                batch(b, False)
            batch(B - 1, True)

        @block.gpsimd
        def _(pool):
            nc.gpsimd.memset(ctT[:, :, :, M:MP].bitcast(F32), 0.0).then_inc(pad_ready, 1)
            nc.gpsimd.memset(bias[:, M:MP], -MASKED / CROSS_SCALE).then_inc(bias_pad, 1)

            def step(at):
                t, tm2 = at(1), at(-2)
                if t is not None and t.par == 0:
                    wait(pool, mask_in, (t.batch + 1) * 16)
                    wait(pool, bias_pad, 1)
                    wait_alone(pool, low_ready, t.batch * 2, passed["pool"])
                    nc.gpsimd.tensor_scalar(bias[:, 0:M], mask8[:], MASKED / CROSS_SCALE, -MASKED / CROSS_SCALE,
                                            ALU.mult, ALU.add).then_inc(bias_ready, 1)
                if tm2 is not None:
                    wait(pool, resid_ready, tm2.count())
                    pool.dma_start(dram["resid"][bass.ds(tm2.index * TS, TS), :], resid[:]).then_inc(resid_out, 16)
                    wait(pool, zT_lo, tm2.count())
                    pool.dma_start(dram["zT"][:, bass.ds(tm2.index, 1)].rearrange("p o h c t -> p (o h) c t"),
                                   zT[:].bitcast(F32)).then_inc(zT_out, 16)
                    wait(pool, v_lo, tm2.count())
                    pool.dma_start(dram["v"][:, :, bass.ds(tm2.index, 1)].rearrange("q p o n -> p q (o n)"),
                                   vout[:].bitcast(F32).rearrange("p (q g) e r -> p q (g e r)", g=2)).then_inc(v_out, 16)
            schedule(pool, step)
            pool.wait_ge(resid_out, 16 * NT)
            pool.wait_ge(zT_out, 16 * NT)
            pool.wait_ge(v_out, 16 * NT)

        @block.tensor
        def _(pe):
            def step(at):
                t, t1, tm1, tm2 = at(0), at(1), at(-1), at(-2)
                if t is not None:
                    wait(pe, pad_ready, 1)
                    wait(pe, xnT_lo, t.count())
                    wait(pe, low_ready, t.count() - 1)
                    for c in range(DC):
                        if t.par == 0:
                            wait(pe, ctT_lo, t.batch * DC + (c + 1))
                        for m in range(2):
                            for i, (u, v) in enumerate(PASSES):
                                last = nc.tensor.matmul(ps_s[0:TS, m, 0:MH], xnT[:, u, c, :], ctT[:, c, v, m * MH:(m + 1) * MH],
                                                        start=(c == 0 and i == 0), stop=(c == DC - 1 and i == 2))
                        last.then_inc(ctT_used, 1)
                if tm1 is not None:
                    wait(pe, exp_done, tm1.count())
                    wait(pe, zT_lo, tm1.count() - 2)
                    for m in range(MC):
                        last = nc.tensor.transpose(ps_t[0][0:MS, m // 3, (m % 3) * TS:(m % 3 + 1) * TS],
                                                   prob[:, tm1.par, m * MS:(m + 1) * MS], keep["ident"][0:TS, 0:TS])
                    last.then_inc(pT_done, 1)
                if t1 is not None:
                    wait(pe, xn_ready, t1.count())
                    wait(pe, v_lo, t1.count() - 4)
                    wait(pe, ha_ready, t1.count() - 4)
                    for c in range(DC):
                        last = nc.tensor.transpose(ps_t[1][:, c // 4, (c % 4) * TS:(c % 4 + 1) * TS],
                                                   xn[:, c * P:(c + 1) * P], keep["ident"][0:TS, 0:TS])
                    last.then_inc(xT_done, 1)
                if tm2 is not None:
                    wait(pe, z_ready, tm2.count())
                    wait(pe, pT_lo, tm2.count() + 1 if tm1 is not None else NT)
                    for c in range(DC):
                        last = nc.tensor.transpose(ps_t[0][:, c // 4, (c % 4) * TS:(c % 4 + 1) * TS],
                                                   z[:, c * P:(c + 1) * P], keep["ident"][0:TS, 0:TS])
                    last.then_inc(zT_done, 1)
                if tm1 is not None:
                    wait(pe, pT_lo, tm1.count())
                    wait(pe, x1_ready, tm1.count() - 1)
                    for m in range(MC):
                        if tm1.par == 0:
                            wait(pe, cx_lo, tm1.batch * MC + (m + 1))
                        for h in range(2):
                            for i, (u, v) in enumerate(PASSES):
                                last = nc.tensor.matmul(ps_r[0:TS, h, :], pT[:, u, m, :], cx[:, m, v, h * 512:(h + 1) * 512],
                                                        start=(m == 0 and i == 0), stop=(m == MC - 1 and i == 2))
                        last.then_inc(cx_used, 1)
                if tm2 is not None:
                    wait(pe, zT_lo, tm2.count())
                    wait(pe, xnT_lo, tm2.count() + 3 if t1 is not None else NT)
                    for c in range(DC):
                        for i, (u, v) in enumerate(PASSES):
                            last = nc.tensor.matmul(ps_t[1][0:TS, 0, 0:VW], zT[:, u, c, :], keep["wvx"][:, v, c, :],
                                                    start=(c == 0 and i == 0), stop=(c == DC - 1 and i == 2))
                    last.then_inc(v_done, 1)
            schedule(pe, step)

        T4 = lambda ps: ps[:, :, 0:4 * TS]
        W4 = lambda buf, u: buf[:, u].rearrange("p (a b) t -> p a (b t)", a=2)

        @block.scalar
        def _(act):
            def ctT_high(b):
                for c in range(DC):
                    wait(act, ctT_in[c % CTR], (b * (DC // CTR) + (c // CTR + 1)) * 16)
                    wait(act, ctT_used, b * (2 * DC) + (c + 1 - DC))
                    nc.scalar.activation(ctT[:, c, 0, 0:M], ctT_raw[:, c % CTR, :], ACT.Copy).then_inc(ctT_hi, 1)

            def cx_high(b):
                for m in range(MC):
                    wait(act, cx_in[m % CXR], (b * (MC // CXR) + (m // CXR + 1)) * 16)
                    wait(act, cx_used, b * (2 * MC) + (m + 1 - MC))
                    nc.scalar.activation(cx[:, m, 0, :], ctx_raw[:, m % CXR, :], ACT.Copy).then_inc(cx_hi, 1)

            def step(at):
                t, t1, tm1, tm2, tm3 = at(0), at(1), at(-1), at(-2), at(-3)
                if t1 is not None and t is None:
                    ctT_high(0)
                if tm2 is not None:
                    wait(act, rsb_ready, tm2.count(2))
                    wait(act, resid_out, (tm2.count() - 1) * 16)
                    nc.scalar.activation(resid[:], xb[:, tm2.par, :], ACT.Identity, bias=res_bias[:],
                                         scale=res_scale[:]).then_inc(resid_ready, 1)
                if tm1 is not None:
                    wait(act, pT_done, tm1.count())
                    wait(act, cx_used, (tm1.count() - 1) * MC)
                    nc.scalar.activation(pT[:, 0].rearrange("p (a b) t -> p a (b t)", a=2),
                                         ps_t[0][0:MS, :, 0:3 * TS], ACT.Copy).then_inc(pT_hi, 1)
                if t1 is not None:
                    wait(act, xT_done, t1.count())
                    wait(act, ctT_used, (t1.count() - 1) * DC)
                    nc.scalar.activation(W4(xnT, 0), T4(ps_t[1]), ACT.Copy).then_inc(xnT_hi, 1)
                if tm2 is not None:
                    wait(act, zT_done, tm2.count())
                    wait(act, v_done, tm2.count() - 1)
                    wait(act, zT_out, (tm2.count() - 1) * 16)
                    nc.scalar.activation(W4(zT, 0), T4(ps_t[0]), ACT.Copy).then_inc(zT_hi, 1)
                if t is not None:
                    wait(act, low_ready, t.count())
                    wait(act, gain_ready, t.count() - 2)
                    nc.scalar.activation(prob[:, t.par, :], prob[:, t.par, :], ACT.Exp, bias=low[:, t.par:t.par + 1],
                                         scale=-1.0, accum_out=total[:, t.par:t.par + 1]).then_inc(exp_done, 1)
                    if t.par == 1 and at(1) is not None:
                        ctT_high(t.batch + 1)
                if tm1 is not None:
                    wait(act, ve_ready, tm1.count())
                    wait(act, rstd_ready, tm1.count() - 1)
                    nc.scalar.activation(std[:], ve[:], ACT.Sqrt).then_inc(std_ready, 1)
                if tm2 is not None:
                    wait(act, v_done, tm2.count())
                    wait(act, v_out, (tm2.count() - 1) * 16)
                    nc.scalar.activation(vout[:, :, 0, :], ps_t[1][0:TS, 0, 0:H * R].rearrange("p (h r) -> p h r", r=R),
                                         ACT.Copy).then_inc(v_hi, 1)
                    nc.scalar.activation(keep["ha"][:, bass.ds(tm2.index, 1), :].rearrange("p o r -> p (o r)"),
                                         ps_t[1][0:TS, 0, H * R:VW], ACT.Copy).then_inc(ha_ready, 1)
                if t is not None and t.par == 0:
                    cx_high(t.batch)
            schedule(act, step)

        @block.vector
        def _(dve):
            def ctT_low(b):
                for c in range(DC):
                    wait(dve, ctT_hi, b * DC + (c + 1))
                    nc.vector.tensor_sub(ctT[:, c, 1, 0:M], ctT_raw[:, c % CTR, :], ctT[:, c, 0, 0:M].bitcast(F32)).then_inc(ctT_lo, 1)

            def cx_low(b):
                for m in range(MC):
                    wait(dve, cx_hi, b * MC + (m + 1))
                    nc.vector.tensor_sub(cx[:, m, 1, :], ctx_raw[:, m % CXR, :], cx[:, m, 0, :].bitcast(F32)).then_inc(cx_lo, 1)

            def norm_x(t):
                wait(dve, xa_in[t.par], (t.batch + 1) * 16)
                wait(dve, xT_done, t.count() - 1)
                nc.vector.tensor_scalar(xn[:], xa[:, t.par, :],
                                        keep["x_mv"][:, bass.ds(t.index, 1), 0],
                                        keep["x_rstd"][:, bass.ds(t.index, 1)],
                                        ALU.subtract, ALU.mult).then_inc(xn_ready, 1)

            def step(at):
                t, t1, t2, tm1, tm2 = at(0), at(1), at(2), at(-1), at(-2)
                if t1 is not None and t is None:
                    norm_x(Tile(0, 0))
                    ctT_low(0)
                if tm2 is not None:
                    wait(dve, std_ready, tm2.count())
                    nc.vector.reciprocal(rstd[:], std[:]).then_inc(rstd_ready, 1)
                    wait(dve, rstd_ready, tm2.count())
                    wait(dve, zT_done, tm2.count() - 1)
                    nc.vector.tensor_scalar(z[:], xb[:, tm2.par, :], mv[:, 0:1], rstd[:, 1:2], ALU.subtract, ALU.mult).then_inc(z_ready, 1)
                    wait(dve, resid_ready, tm2.count() - 1)
                    nc.vector.tensor_scalar(res_scale[:], rstd[:, 0:1], 1.0, None, ALU.add).then_inc(rsb_ready, 1)
                    nc.vector.tensor_scalar(res_bias[:], mv[:, 0:1], rstd[:, 0:1], -1.0, ALU.mult, ALU.mult).then_inc(rsb_ready, 1)
                if tm1 is not None:
                    wait(dve, pT_hi, tm1.count())
                    nc.vector.tensor_tensor(pT[:, 1].rearrange("p (a b) t -> p a (b t)", a=2), ps_t[0][0:MS, :, 0:3 * TS],
                                            pT[:, 0].rearrange("p (a b) t -> p a (b t)", a=2).bitcast(F32), ALU.subtract).then_inc(pT_lo, 1)
                if t is not None:
                    wait(dve, ctT_used, t.count() * DC)
                    wait(dve, bias_ready, t.batch + 1)
                    wait(dve, bias_pad, 1)
                    wait_alone(dve, pT_done, t.count() - 2, passed["dve"])
                    nc.vector.tensor_tensor_reduce(out=prob[:, t.par, :].rearrange("p (a m) -> p a m", a=2),
                                                   in0=ps_s[0:TS, :, 0:MH], in1=bias[:].rearrange("p (a m) -> p a m", a=2),
                                                   scale=-CROSS_SCALE, scalar=FAR, op0=ALU.add, op1=ALU.min,
                                                   accum_out=low[:, t.par:t.par + 1]).then_inc(low_ready, 1)
                if t1 is not None:
                    wait(dve, xnT_hi, t1.count())
                    nc.vector.tensor_tensor(W4(xnT, 1), T4(ps_t[1]), W4(xnT, 0).bitcast(F32), ALU.subtract).then_inc(xnT_lo, 1)
                if tm2 is not None:
                    wait(dve, zT_hi, tm2.count())
                    nc.vector.tensor_tensor(W4(zT, 1), T4(ps_t[0]), W4(zT, 0).bitcast(F32), ALU.subtract).then_inc(zT_lo, 1)
                if t is not None and t.par == 1 and t1 is not None:
                    ctT_low(t.batch + 1)
                if tm1 is not None:
                    wait(dve, exp_done, tm1.count())
                    nc.vector.reciprocal(rinv[:], total[:, tm1.par:tm1.par + 1]).then_inc(rinv_ready, 1)
                    wait(dve, rinv_ready, tm1.count())
                    nc.vector.tensor_scalar(gain[:], rinv[:], keep["valid"][:, bass.ds(tm1.batch, 1)], None, ALU.mult).then_inc(gain_ready, 1)
                    wait(dve, gain_ready, tm1.count())
                    wait(dve, xb_in[tm1.par], (tm1.batch + 1) * 16)
                    wait(dve, cx_used, tm1.count() * MC)
                    x1 = xb[:, tm1.par, :].rearrange("p (a n) -> p a n", a=2)
                    nc.vector.scalar_tensor_tensor(out=x1, in0=ps_r[0:TS], scalar=gain[:], in1=x1, op0=ALU.mult, op1=ALU.add).then_inc(x1_ready, 1)
                    wait(dve, x1_ready, tm1.count())
                    for i in range(2):
                        nc.vector.bn_stats(stats[:, i, :], xb[:, tm1.par, i * 512:(i + 1) * 512]).then_inc(st_ready, 1)
                    wait(dve, st_ready, tm1.count(2))
                    wait(dve, rsb_ready, tm1.count(2) - 2)
                    wait_alone(dve, z_ready, tm1.count() - 1, passed["dve"])
                    nc.vector.bn_aggr(mv[:], stats[:]).then_inc(mv_ready, 1)
                    wait(dve, mv_ready, tm1.count())
                    nc.vector.tensor_scalar(ve[:, 0:1], mv[:, 1:2], LN_EPS, None, ALU.add).then_inc(ve_half, 1)
                    wait(dve, ve_half, tm1.count())
                    nc.vector.scalar_tensor_tensor(out=ve[:, 1:2], in0=ve[:, 0:1], scalar=RMS_EPS, in1=mv[:, 1:2],
                                                   op0=ALU.mult, op1=ALU.add).then_inc(ve_ready, 1)
                if tm2 is not None:
                    wait(dve, v_hi, tm2.count())
                    wait(dve, ha_ready, tm2.count())
                    nc.vector.tensor_tensor(vout[:, :, 1, :], ps_t[1][0:TS, 0, 0:H * R].rearrange("p (h r) -> p h r", r=R),
                                            vout[:, :, 0, :].bitcast(F32), ALU.subtract).then_inc(v_lo, 1)
                if t2 is not None:
                    norm_x(t2)
                if t is not None and t.par == 0:
                    cx_low(t.batch)
            schedule(dve, step)


def self_attention(nc, dram, keep):
    ctx = ExitStack()
    with ctx:
        sb = lambda n, s, d=F32: ctx.enter_context(nc.sbuf_tensor(n, s, d))
        pb = lambda n, s: ctx.enter_context(nc.psum_tensor(n, s, F32))
        sem = lambda n: ctx.enter_context(nc.semaphore(n))
        UNITS = 4
        STEPS = HP * NB
        zz = sb("zz", [P, NT, 2, DC, TS], F32R)
        w_raw = sb("w_raw", [P, 2, DC, P])
        w = sb("w", [P, 2, 2, 2, DC, P], F32R)
        qk = sb("qk", [P, 2, 2, 2, BW], F32R)
        vb = sb("vb", [TS, 2, NT, 2, 2 * R], F32R)
        prob = sb("prob2", [TS, UNITS, 2, S])
        probT = sb("probT", [TS, 2, 2, 4, TS], F32R)
        acc = sb("acc", [2 * R, T])
        low = sb("low2", [TS, UNITS, 2])
        total = sb("total2", [TS, UNITS, 2])
        rinv = sb("rinv2", [TS, UNITS, 2])
        sums = sb("sums", [TS, NT, 2 * R])
        mod = sb("mod", [TS, NT, R])
        u = sb("u", [TS, NT, R])
        u3 = prob[:].rearrange("p u q k -> p (u q k)")[:, 0:NT * 96].rearrange("p (t n) -> p t n", n=96)
        u_hi = sb("u_hi", [TS, NT, R], F32R)
        uT = qk[0:96].rearrange("p a b c n -> p (a b c n)")[:, 0:T]
        ps_p = [pb("ps_q", [P, 512]), pb("ps_k", [P, 512])]
        ps_s = [pb("ps_s0", [P, 512]), pb("ps_s1", [P, 512])]
        ps_t = [pb("ps_pt0", [P, 512]), pb("ps_pt1", [P, 512])]
        ps_o = [pb("ps_o0", [P, 512]), pb("ps_o1", [P, 512])]
        zz_in = [sem(f"zz_in{i}") for i in range(NB)]
        w_in = [sem("wq_in"), sem("wk_in")]
        vb_in = [sem("vb_in0"), sem("vb_in1")]
        w_scaled, w_hi, w_lo, proj_done, qk_hi, qk_lo = (sem(n) for n in ("w_scaled", "w_hi", "w_lo", "proj_done", "qk_hi", "qk_lo"))
        s_done, low_ready, exp_done, rinv_ready, prob_ready = (sem(n) for n in ("s_done", "low_ready2", "exp_done2", "rinv_ready2", "prob_ready"))
        pt_done, pt_hi, pt_lo, pv_done, o_added, zeroed, acc_zero = (sem(n) for n in ("pt_done", "pt_hi", "pt_lo", "pv_done", "o_added", "zeroed", "acc_zero"))
        sums_done, sums_ready, attn_ready, mod_ready, u_ready, u3_zero, u3_part, u3_ready, uT_done, uT_ready = (
            sem(n) for n in ("sums_done", "sums_ready", "attn_ready", "mod_ready", "u_ready", "u3_zero", "u3_part", "u3_ready", "uT_done", "uT_ready"))
        uT_out = sem("uT_out")
        passed = {n: sem("passed_" + n) for n in ("sp", "pool", "dve")}
        block = ctx.enter_context(nc.Block())

        class Unit:

            def __init__(self, pair, x):
                self.pair = pair + x // 16 if x // 16 else pair
                self.x = x % 16
                self.blk, self.u = self.x // UNITS, self.x % UNITS
                self.bi, self.head = self.u // 2, self.u % 2
                self.spar = self.blk % 2

            @property
            def count(self):
                return self.pair * 16 + (self.x + 1)

            def step(self, off=0):
                return self.pair * NB + (self.blk + off)

        def schedule(eng, quarter):
            def run(pair, ppar, x, steady):
                def at(k):
                    n = x + k
                    if not (steady or 0 <= 16 * pair + n < 16 * HP):
                        return None, 0
                    return Unit(pair, n), (ppar + n // 16) % 2
                quarter(pair if steady or pair < HP else None, ppar, x, at)
            for x in range(16):
                run(0, 0, x, False)
            for x in range(16):
                run(1, 1, x, True)
            with eng.Fori(2, HP - 1, 2) as pair:
                for x in range(16):
                    run(pair, 0, x, True)
                for x in range(16):
                    run(pair + 1, 1, x, True)
            for x in range(UNITS + 3):
                run(HP, 0, x, False)

        SC, PT, PV = -UNITS, -UNITS - 2, -UNITS - 3

        @block.sync
        def _(sp):
            def load_w(pair, source=None):
                for i, name in enumerate(("wq", "wk")):
                    wait_alone(sp, w_lo, pair * 2 + (i - 1), passed["sp"])
                    sp.dma_start(w_raw[:, i], dram[name][bass.ds(pair if source is None else source, 1)].rearrange("o p c n -> p (o c) n")).then_inc(w_in[i], 16)

            def load_v(pair, ppar):
                wait_alone(sp, pv_done, (pair - 1) * 16, passed["sp"])
                sp.dma_start(vb[:, ppar].bitcast(F32).rearrange("p t g n -> p t (g n)"),
                             dram["v"][bass.ds(pair, 1)].rearrange("o p t n -> p (o t) n")).then_inc(vb_in[ppar], 16)

            load_w(0)
            for i in range(NB):
                sp.dma_start(zz[:, i * BT:(i + 1) * BT].bitcast(F32), dram["zT"][:, i * BT:(i + 1) * BT]).then_inc(zz_in[i], 16)
            load_w(1)
            load_v(0, 0)
            load_v(1, 1)
            with sp.Fori(2, HP - 1, 2) as pair:
                load_w(pair)
                load_v(pair, 0)
                load_w(pair + 1)
                load_v(pair + 1, 1)
            load_w(HP, 0)
            sp.wait_ge(uT_ready, NB)
            sp.dma_start(dram["uT"], uT.bitcast(F32)).then_inc(uT_out, 16)
            sp.wait_ge(uT_out, 16)

        @block.tensor
        def _(pe):
            def quarter(pair, ppar, x, at):
                blk, q = x // 4, x % 4
                if pair is not None:
                    i, half = q // 2, q % 2
                    if half == 0:
                        if isinstance(pair, int) and pair == 0:
                            wait(pe, zz_in[blk], 16)
                        if blk == 0:
                            wait(pe, w_lo, pair * 2 + (i + 1))
                        wait(pe, qk_lo, pair * (2 * NB) + (2 * blk + i - 1))
                    for c in range(half * DC // 2, (half + 1) * DC // 2):
                        for n, (a, b) in enumerate(PASSES):
                            last = nc.tensor.matmul(ps_p[i][:, 0:BW], w[:, ppar, i, a, c, :], zz[:, blk * BT:(blk + 1) * BT, b, c, :],
                                                    start=(c == 0 and n == 0), stop=(c == DC - 1 and n == 2))
                    if half:
                        last.then_inc(proj_done, 1)
                s, _ = at(SC)
                if s is not None:
                    if s.u == 0:
                        wait(pe, qk_lo, s.step(1) * 2)
                    wait(pe, low_ready, (s.count - 2) * 2)
                    rows = slice(s.head * HD, (s.head + 1) * HD)
                    for qt in range(2):
                        for n, (a, b) in enumerate(PASSES):
                            last = nc.tensor.matmul(ps_s[s.u % 2][0:TS, qt * S:(qt + 1) * S],
                                                    qk[rows, s.spar, 0, a, s.bi * S + qt * TS:s.bi * S + (qt + 1) * TS],
                                                    qk[rows, s.spar, 1, b, s.bi * S:(s.bi + 1) * S],
                                                    start=(n == 0), stop=(n == 2))
                    last.then_inc(s_done, 1)
                t, _ = at(PT)
                if t is not None:
                    wait(pe, prob_ready, t.count * 2)
                    wait(pe, pt_lo, t.count - 2)
                    for n, (qt, kt) in enumerate(((0, 0), (1, 0), (1, 1))):
                        last = nc.tensor.transpose(ps_t[t.u % 2][0:TS, n * TS:(n + 1) * TS],
                                                   prob[:, t.u, qt, kt * TS:(kt + 1) * TS], keep["ident"][0:TS, 0:TS])
                    last.then_inc(pt_done, 1)
                v, vpar = at(PV)
                if v is not None:
                    wait(pe, pt_lo, v.count)
                    if v.x == 0:
                        wait(pe, vb_in[vpar], (v.pair - vpar) * 8 + 16)
                    if v.head == 0:
                        wait(pe, o_added, v.pair * 8 + (v.x // 2 - 1))
                    for n, (kt, b) in enumerate(((0, 0), (1, 0), (0, 1), (1, 1))):
                        last = nc.tensor.matmul(ps_o[v.bi][0:2 * R, 0:S],
                                                vb[:, vpar, v.blk * BT + v.bi * 2 + kt, v.head, :],
                                                probT[:, v.u % 2, b, (1 - kt):(3 if kt == 0 else 4):(1 if kt == 0 else 3), :],
                                                start=(v.head == 0 and n == 0), stop=(v.head == 1 and n == 3))
                    last.then_inc(pv_done, 1)
            schedule(pe, quarter)
            pe.wait_ge(o_added, 8 * HP)
            for t in range(NT):
                last = nc.tensor.transpose(ps_s[0][0:TS, t * 2 * R:(t + 1) * 2 * R], acc[:, t * TS:(t + 1) * TS],
                                           keep["ident"][0:2 * R, 0:2 * R])
            last.then_inc(sums_done, 1)
            pe.wait_ge(u3_ready, 3)
            for t in range(NT):
                if t % BT == 0:
                    wait(pe, uT_ready, t // BT - 1)
                last = nc.tensor.transpose(ps_p[t // BT % 2][0:96, t % BT * TS:(t % BT + 1) * TS], u3[:, t, :],
                                           keep["ident"][0:TS, 0:TS])
                if t % BT == BT - 1:
                    last.then_inc(uT_done, 1)

        @block.scalar
        def _(act):
            def split_high(pair, ppar, i):
                wait(act, w_scaled, pair * 2 + (i + 1))
                wait(act, proj_done, (pair - 1) * (2 * NB))
                nc.scalar.activation(w[:, ppar, i, 0], w_raw[:, i], ACT.Copy).then_inc(w_hi, 1)

            def quarter(pair, ppar, x, at):
                blk, q = x // 4, x % 4
                if pair is not None and q % 2 == 1:
                    i = q // 2
                    wait(act, proj_done, pair * (2 * NB) + (2 * blk + i + 1))
                    wait(act, s_done, pair * 16 + (blk - 1) * 4)
                    nc.scalar.activation(qk[:, blk % 2, i, 0], ps_p[i][:, 0:BW], ACT.Copy).then_inc(qk_hi, 1)
                t, _ = at(PT)
                if t is not None:
                    wait(act, pt_done, t.count)
                    wait(act, zeroed, 2)
                    wait(act, pv_done, t.count - 2)
                    nc.scalar.activation(probT[:, t.u % 2, 0, 1:4, :].rearrange("p b t -> p (b t)"),
                                         ps_t[t.u % 2][0:TS, 0:3 * TS], ACT.Copy).then_inc(pt_hi, 1)
                s, _ = at(SC)
                if s is not None:
                    wait(act, rinv_ready, s.count - UNITS)
                    for qt in range(2):
                        wait(act, low_ready, (s.count - 1) * 2 + (qt + 1))
                        kw = (qt + 1) * TS
                        nc.scalar.activation(prob[:, s.u, qt, 0:kw], prob[:, s.u, qt, 0:kw], ACT.Exp,
                                             bias=low[:, s.u, qt:qt + 1], scale=-1.0,
                                             accum_out=total[:, s.u, qt:qt + 1]).then_inc(exp_done, 1)
                if pair is not None and x in (4, 6):
                    split_high(pair + 1, 1 - ppar, (x - 4) // 2)

            split_high(0, 0, 0)
            split_high(0, 0, 1)
            schedule(act, quarter)
            act.wait_ge(attn_ready, 1)
            nc.scalar.activation(mod[:], mod[:], ACT.Tanh).then_inc(mod_ready, 1)
            for i in range(NB):
                act.wait_ge(uT_done, i + 1)
                nc.scalar.activation(uT[:, i * BW:(i + 1) * BW], ps_p[i % 2][0:96, 0:BW], ACT.Copy).then_inc(uT_ready, 1)

        @block.gpsimd
        def _(pool):
            nc.gpsimd.memset(probT[:, 0, :, 0, :].bitcast(F32), 0.0).then_inc(zeroed, 1)
            nc.gpsimd.memset(probT[:, 1, :, 0, :].bitcast(F32), 0.0).then_inc(zeroed, 1)

            def scale(pair):
                for i in range(2):
                    wait(pool, w_in[i], pair * 16 + 16)
                    nc.gpsimd.tensor_tensor(w_raw[:, i], w_raw[:, i], keep["ln1"][:].unsqueeze(2).to_broadcast([P, DC, P]),
                                            ALU.mult).then_inc(w_scaled, 1)

            scale(0)
            with pool.Fori(1, HP + 1) as pair:
                scale(pair)

        @block.vector
        def _(dve):
            def split_low(pair, ppar, i):
                wait(dve, w_hi, pair * 2 + (i + 1))
                nc.vector.tensor_sub(w[:, ppar, i, 1], w_raw[:, i], w[:, ppar, i, 0].bitcast(F32)).then_inc(w_lo, 1)

            def quarter(pair, ppar, x, at):
                blk, q = x // 4, x % 4
                if pair is not None and q % 2 == 1:
                    i = q // 2
                    wait(dve, qk_hi, pair * (2 * NB) + (2 * blk + i + 1))
                    nc.vector.tensor_tensor(qk[:, blk % 2, i, 1], ps_p[i][:, 0:BW], qk[:, blk % 2, i, 0].bitcast(F32),
                                            ALU.subtract).then_inc(qk_lo, 1)
                s, _ = at(SC)
                if s is not None:
                    wait(dve, s_done, s.count)
                    wait(dve, acc_zero, 1)
                    wait_alone(dve, pt_done, s.count - UNITS, passed["dve"])
                    for qt in range(2):
                        kw = (qt + 1) * TS
                        nc.vector.tensor_tensor_reduce(out=prob[:, s.u, qt, 0:kw], in0=ps_s[s.u % 2][0:TS, qt * S:qt * S + kw],
                                                       in1=keep["causal"][:, S - kw:S], scale=-SELF_SCALE, scalar=FAR,
                                                       op0=ALU.add, op1=ALU.min,
                                                       accum_out=low[:, s.u, qt:qt + 1]).then_inc(low_ready, 1)
                t, _ = at(PT)
                if t is not None:
                    wait(dve, pt_hi, t.count)
                    nc.vector.tensor_tensor(probT[:, t.u % 2, 1, 1:4, :].rearrange("p b t -> p (b t)"),
                                            ps_t[t.u % 2][0:TS, 0:3 * TS],
                                            probT[:, t.u % 2, 0, 1:4, :].rearrange("p b t -> p (b t)").bitcast(F32),
                                            ALU.subtract).then_inc(pt_lo, 1)
                v, _ = at(PV)
                if v is not None and v.head == 1:
                    wait(dve, pv_done, v.count)
                    wait(dve, acc_zero, 1)
                    cols = slice((v.blk * BT + v.bi * 2) * TS, (v.blk * BT + v.bi * 2 + 2) * TS)
                    nc.vector.tensor_tensor(acc[:, cols], ps_o[v.bi][0:2 * R, 0:S], acc[:, cols], ALU.add).then_inc(o_added, 1)
                if s is not None:
                    wait(dve, exp_done, s.count * 2)
                    nc.vector.reciprocal(rinv[:, s.u], total[:, s.u]).then_inc(rinv_ready, 1)
                    wait(dve, rinv_ready, s.count)
                    for qt in range(2):
                        kw = (qt + 1) * TS
                        nc.vector.tensor_scalar(prob[:, s.u, qt, 0:kw], prob[:, s.u, qt, 0:kw], rinv[:, s.u, qt:qt + 1],
                                                None, ALU.mult).then_inc(prob_ready, 1)
                if pair is not None and x in (4, 6):
                    split_low(pair + 1, 1 - ppar, (x - 4) // 2)

            nc.vector.memset(acc[:], 0.0).then_inc(acc_zero, 1)
            split_low(0, 0, 0)
            split_low(0, 0, 1)
            schedule(dve, quarter)
            dve.wait_ge(sums_done, 1)
            nc.vector.memset(u3, 0.0).then_inc(u3_zero, 1)
            nc.vector.tensor_copy(sums[:].rearrange("p t r -> p (t r)"), ps_s[0][0:TS, :]).then_inc(sums_ready, 1)
            dve.wait_ge(sums_ready, 1)
            nc.vector.tensor_tensor(mod[:], sums[:, :, 0:R], sums[:, :, R:2 * R], ALU.add).then_inc(attn_ready, 1)
            dve.wait_ge(mod_ready, 1)
            nc.vector.scalar_tensor_tensor(out=u[:], in0=mod[:], scalar=MOD_SCALE, in1=keep["ha"][:], op0=ALU.mult,
                                           op1=ALU.mult).then_inc(u_ready, 1)
            dve.wait_ge(u_ready, 1)
            nc.vector.tensor_copy(u_hi[:], u[:]).then_inc(u3_part, 1)
            dve.wait_ge(u3_part, 1)
            dve.wait_ge(u3_zero, 1)
            for i in range(2):
                nc.vector.tensor_copy(u3[:, :, 32 * i:32 * i + R], u_hi[:].bitcast(F32)).then_inc(u3_ready, 1)
            nc.vector.tensor_sub(u3[:, :, 64:64 + R], u[:], u_hi[:].bitcast(F32)).then_inc(u3_ready, 1)


def ffn(nc, dram, keep):
    ctx = ExitStack()
    with ctx:
        sb = lambda n, s, d=F32: ctx.enter_context(nc.sbuf_tensor(n, s, d))
        pb = lambda n, s: ctx.enter_context(nc.psum_tensor(n, s, F32))
        sem = lambda n: ctx.enter_context(nc.semaphore(n))
        HT = T // 2
        BLK = HT // BW
        JT = HT // P
        G = 4
        zh = sb("zh", [P, NT // 2, 2, DC, TS], F32R)
        gu_raw = sb("gu_raw", [P, 2, DC, P])
        gu = sb("gu", [P, 2, 2, 2, DC, P], F32R)
        wd_raw = sb("wd_raw", [P, D])
        wd = sb("wd", [P, G, 2, D], F32R)
        bs = sb("bs", [96, 2, P], F32R)
        uh = sb("uh", [96, HT], F32R)
        gate = sb("gate", [P, 2, BW])
        prod = sb("prod", [P, 2, BW])
        hid = sb("hid", [P, G, 2, HT], F32R)
        acc = sb("out_acc", [P, JT, D])
        ps_g = [pb("ps_g0", [P, 512]), pb("ps_g1", [P, 512])]
        ps_u = [pb("ps_u0", [P, 512]), pb("ps_u1", [P, 512])]
        ps_d = [pb(f"ps_d{i}", [P, 512]) for i in range(4)]
        zh_in = [sem("zh_in0"), sem("zh_in1")]
        uh_in, acc_in = sem("uh_in"), sem("acc_in")
        gu_in = [sem("g_in"), sem("u_in")]
        wd_in = sem("wd_in")
        bs_in = [sem("bs_in0"), sem("bs_in1")]
        gu_scaled, gu_hi, gu_lo, wd_hi, wd_lo = (sem(n) for n in ("gu_scaled", "gu_hi", "gu_lo", "wd_hi", "wd_lo"))
        gate_done, up_done, silu_ready, prod_ready, hid_hi, hid_lo, down_done, added, out_done = (
            sem(n) for n in ("gate_done", "up_done", "silu_ready", "prod_ready", "hid_hi", "hid_lo", "down_done", "added", "out_done"))
        ADDS = JT * 2
        passed = {n: sem("passed_" + n) for n in ("sp", "pool", "dve")}
        block = ctx.enter_context(nc.Block())

        def schedule(eng, step, down):
            def turn(base, half, first):
                for k in range(G):
                    step(base + k, k, half)
                    if k % 2 == 0 and not (first and k == 0):
                        down(base + (k - 2), (k - 2) % G, half)
            for half in range(2):
                turn(half * NF, half, True)
                with eng.Fori(half * NF + G, (half + 1) * NF - G + 1, G) as base:
                    turn(base, half, False)
                down((half + 1) * NF - 2, G - 2, half)

        @block.sync
        def _(sp):
            def load(n, f, k):
                for i, name in enumerate(("w_in", "w_up")):
                    wait_alone(sp, gu_lo, n * 2 + (i - 1), passed["sp"])
                    sp.dma_start(gu_raw[:, i], dram[name][bass.ds(f, 1)].rearrange("o p c n -> p (o c) n")).then_inc(gu_in[i], 16)
                wait_alone(sp, gate_done, (n - 1) * BLK, passed["sp"])
                sp.dma_start(bs[:, k % 2].bitcast(F32), dram["b_stack"][bass.ds(f, 1)].rearrange("o k n -> (o k) n")).then_inc(bs_in[k % 2], 16)
                wait_alone(sp, wd_lo, n, passed["sp"])
                sp.dma_start(wd_raw[:], dram["w_down"][bass.ds(f, 1)].rearrange("o p d -> (o p) d")).then_inc(wd_in, 16)

            for half in range(2):
                rows = slice(half * HT, (half + 1) * HT)
                load(half * NF, 0, 0)
                wait(sp, up_done, half * NF * BLK)
                for i in range(BLK):
                    sp.dma_start(zh[:, i * BT:(i + 1) * BT].bitcast(F32),
                                 dram["zT"][:, (half * BLK + i) * BT:(half * BLK + i + 1) * BT]).then_inc(zh_in[i], 16)
                sp.dma_start(uh[:].bitcast(F32), dram["uT"][:, rows]).then_inc(uh_in, 16)
                load(half * NF + 1, 1, 1)
                if half:
                    sp.wait_ge(added, NF // 2 * ADDS)
                    sp.dma_start(dram["out"][0:HT, :].rearrange("(j p) d -> p j d", p=P), acc[:]).then_inc(out_done, 16)
                    sp.wait_ge(out_done, 16)
                sp.dma_start(acc[:], dram["resid"][rows, :].rearrange("(j p) d -> p j d", p=P)).then_inc(acc_in, 16)
                for k in range(2, G):
                    load(half * NF + k, k, k)
                with sp.Fori(G, NF - G + 1, G) as f:
                    for k in range(G):
                        load(f + (half * NF + k), f + k, k)
            load(2 * NF, 0, 0)
            sp.wait_ge(added, NF * ADDS)
            sp.dma_start(dram["out"][HT:T, :].rearrange("(j p) d -> p j d", p=P), acc[:]).then_inc(out_done, 16)
            sp.wait_ge(out_done, 32)

        @block.gpsimd
        def _(pool):
            def scale(n):
                for i in range(2):
                    wait(pool, gu_in[i], n * 16 + 16)
                    nc.gpsimd.tensor_tensor(gu_raw[:, i], gu_raw[:, i], keep["ln2"][:].unsqueeze(2).to_broadcast([P, DC, P]),
                                            ALU.mult).then_inc(gu_scaled, 1)
            scale(0)
            with pool.Fori(1, 2 * NF + 1) as n:
                scale(n)

        @block.tensor
        def _(pe):
            def step(n, k, half):
                wait(pe, gu_lo, n * 2 + 2)
                wait(pe, bs_in[k % 2], n * 8 + (2 - k % 2) * 8)
                if k == 0:
                    wait(pe, uh_in, (half + 1) * 16)
                for b in range(BLK):
                    if k == 0:
                        wait(pe, zh_in[b], (half + 1) * 16)
                    z = lambda part, c: zh[:, b * BT:(b + 1) * BT, part, c, :]
                    wait(pe, silu_ready, n * BLK + (b - 1))
                    for c in range(DC):
                        for i, (u, v) in enumerate(PASSES):
                            nc.tensor.matmul(ps_g[b][:, 0:BW], gu[:, k % 2, 0, u, c, :], z(v, c), start=(c == 0 and i == 0), stop=False)
                    nc.tensor.matmul(ps_g[b][:, 0:BW], bs[:, k % 2, :], uh[:, b * BW:(b + 1) * BW], start=False, stop=True).then_inc(gate_done, 1)
                    wait(pe, prod_ready, n * BLK + (b - 1))
                    for c in range(DC):
                        for i, (u, v) in enumerate(PASSES):
                            last = nc.tensor.matmul(ps_u[b][:, 0:BW], gu[:, k % 2, 1, u, c, :], z(v, c),
                                                    start=(c == 0 and i == 0), stop=(c == DC - 1 and i == 2))
                    last.then_inc(up_done, 1)

            def down(n, k, half):
                wait(pe, wd_lo, n + 2)
                wait(pe, hid_lo, n * BLK + 2 * BLK)
                for at in range(ADDS):
                    j, h = at // 2, at % 2
                    wait(pe, added, n * JT + (at - 3))
                    for g in range(2):
                        for i, (u, v) in enumerate(PASSES):
                            last = nc.tensor.matmul(ps_d[(k // 2 * ADDS + at) % 4][:], hid[:, k + g, u, j * P:(j + 1) * P],
                                                    wd[:, k + g, v, h * 512:(h + 1) * 512],
                                                    start=(g == 0 and i == 0), stop=(g == 1 and i == 2))
                    last.then_inc(down_done, 1)
            schedule(pe, step, down)

        @block.scalar
        def _(act):
            def split(n, k):
                for i in range(2):
                    wait(act, gu_scaled, n * 2 + (i + 1))
                    wait(act, up_done if i else gate_done, (n - 1) * BLK)
                    nc.scalar.activation(gu[:, k % 2, i, 0], gu_raw[:, i], ACT.Copy).then_inc(gu_hi, 1)

            def split_down(n, k):
                wait(act, wd_in, n * 16 + 16)
                wait(act, down_done, n * JT - (k % 2 + 2) * JT)
                nc.scalar.activation(wd[:, k, 0], wd_raw[:], ACT.Copy).then_inc(wd_hi, 1)

            def step(n, k, half):
                split(n + 1, (k + 1) % G)
                for b in range(BLK):
                    wait(act, gate_done, n * BLK + (b + 1))
                    wait(act, prod_ready, n * BLK + (b - 1))
                    nc.scalar.activation(gate[:, b], ps_g[b][:, 0:BW], ACT.Silu).then_inc(silu_ready, 1)
                    if b == 0:
                        split_down(n + 1, (k + 1) % G)
                    wait(act, prod_ready, n * BLK + (b + 1))
                    wait(act, down_done, n * JT - (k % 2 + 2) * JT)
                    nc.scalar.activation(hid[:, k, 0, b * BW:(b + 1) * BW], prod[:, b], ACT.Copy).then_inc(hid_hi, 1)
            split(0, 0)
            split_down(0, 0)
            schedule(act, step, lambda *a: None)

        @block.vector
        def _(dve):
            def split(n, k):
                for i in range(2):
                    wait(dve, gu_hi, n * 2 + (i + 1))
                    nc.vector.tensor_sub(gu[:, k % 2, i, 1], gu_raw[:, i], gu[:, k % 2, i, 0].bitcast(F32)).then_inc(gu_lo, 1)

            def split_down(n, k):
                wait(dve, wd_hi, n + 1)
                nc.vector.tensor_sub(wd[:, k, 1], wd_raw[:], wd[:, k, 0].bitcast(F32)).then_inc(wd_lo, 1)

            def step(n, k, half):
                split(n + 1, (k + 1) % G)
                for b in range(BLK):
                    wait(dve, up_done, n * BLK + (b + 1))
                    wait(dve, silu_ready, n * BLK + (b + 1))
                    wait(dve, hid_lo, n * BLK + (b - 1))
                    nc.vector.tensor_tensor(prod[:, b], gate[:, b], ps_u[b][:, 0:BW], ALU.mult).then_inc(prod_ready, 1)
                    if b == 0:
                        split_down(n + 1, (k + 1) % G)
                    wait(dve, hid_hi, n * BLK + (b + 1))
                    nc.vector.tensor_sub(hid[:, k, 1, b * BW:(b + 1) * BW], prod[:, b],
                                         hid[:, k, 0, b * BW:(b + 1) * BW].bitcast(F32)).then_inc(hid_lo, 1)

            def down(n, k, half):
                dve.wait_ge(acc_in, (half + 1) * 16)
                for at in range(ADDS):
                    j, h = at // 2, at % 2
                    wait(dve, down_done, n * JT + (at + 1))
                    part = acc[:, j, h * 512:(h + 1) * 512]
                    nc.vector.tensor_tensor(part, ps_d[(k // 2 * ADDS + at) % 4][:], part, ALU.add).then_inc(added, 1)
            split(0, 0)
            split_down(0, 0)
            schedule(dve, step, down)


def program(nc, dram):
    ctx = ExitStack()
    with ctx:
        sb = lambda n, s, d=F32: ctx.enter_context(nc.sbuf_tensor(n, s, d))
        dr = lambda n, s, d=F32: nc.dram_tensor(n, s, d, kind="Internal").ap()
        dram = dict(dram)
        dram["zT"] = dr("zT_dram", (P, NT, 2, DC, TS))
        dram["v"] = dr("v_dram", (HP, TS, NT, 4 * R))
        dram["resid"] = dr("resid_dram", (T, D))
        dram["b_stack"] = dr("b_stack_dram", (NF, 96, P))
        dram["uT"] = dr("uT_dram", (96, T))
        keep = {
            "ident": sb("ident", [P, P]),
            "causal": sb("causal", [TS, S]),
            "ln1": sb("ln1", [P, DC]),
            "ln2": sb("ln2", [P, DC]),
            "ha": sb("ha", [TS, NT, R]),
        }
        with ExitStack() as inner:
            for n, s, d in (("wvx", [P, 2, DC, VW], F32R), ("x_mv", [TS, NT, 2], F32), ("x_rstd", [TS, NT], F32), ("valid", [TS, B], F32)):
                keep[n] = inner.enter_context(nc.sbuf_tensor("keep_" + n, s, d))
            fold(nc, dram, keep)
            cross(nc, dram, keep)
        self_attention(nc, dram, keep)
        ffn(nc, dram, keep)


def kernel(**inputs):
    import numpy as np
    import concourse.bacc as bacc
    from concourse.bass_utils import run_bass_kernel_spmd

    a = {k: np.asarray(v) for k, v in inputs.items()}
    columns = lambda w, n: w.reshape(n, P, DC, P).transpose(0, 3, 2, 1)
    laid = {
        "x": a["x"].reshape(T, D),
        "ctx": a["ctx_2048"].reshape(B, MC, MS, D),
        "ctxT": a["ctx_2048"].transpose(0, 2, 1).reshape(B, DC, P, M),
        "mask": a["mask_BxS2_bk0"],
        "ln1": a["L0_ffn_ln1_w"].reshape(DC, P).T,
        "ln2": a["L0_ffn_ln2_w"].reshape(DC, P).T,
        "wq": columns(a["L0_ffn_Wq"], HP),
        "wk": columns(a["L0_ffn_Wk"], HP),
        "wv": a["L0_ffn_Wv"],
        "wo": a["L0_ffn_Wo"],
        "a": a["L0_ffn_A"],
        "b": a["L0_ffn_B"],
        "w_in": columns(a["L0_ffn_W_in_base"], NF),
        "w_up": columns(a["L0_ffn_W_up_base"], NF),
        "w_down": a["L0_ffn_W_down"].T.reshape(NF, P, D),
    }
    laid = {k: np.ascontiguousarray(v) for k, v in laid.items()}
    nc = bacc.Bacc("TRN2", target_bir_lowering=False, num_devices=1)
    dram = {k: nc.dram_tensor("in_" + k, v.shape, mybir.dt.from_np(v.dtype), kind="ExternalInput").ap() for k, v in laid.items()}
    dram["out"] = nc.dram_tensor("out", (T, D), F32, kind="ExternalOutput").ap()
    program(nc, dram)
    r = run_bass_kernel_spmd(nc, [{"in_" + k: v for k, v in laid.items()}], core_ids=[0])
    return r.results[0]["out"].reshape(B, S, D)
```

```python
from contextlib import ExitStack

import concourse.bass as bass
from concourse import mybir
from concourse.alu_op_type import AluOpType as ALU

F32 = mybir.dt.float32
F32R = mybir.dt.float32r
U8 = mybir.dt.uint8
ACT = mybir.ActivationFunctionType
AX = mybir.AxisListType

B, S, D, M = 8, 224, 1024, 750
FF, R, H, HD = 4096, 16, 16, 64
P = 128
T = B * S
TS = 112
NT = T // TS
DC = D // P
MC, MS = 6, M // 6
MH = -(-M // 4) * 2
MP = 2 * MH
HP = H // 2
NB = 4
BT = NT // NB
BW = T // NB
VW = H * R + R
NF = FF // P
LN_EPS, RMS_EPS = 1e-5, 1e-6
MOD_SCALE = 0.1
CROSS_SCALE = 1.0 / 32.0
SELF_SCALE = 1.0 / 8.0
MASKED = 1e30
FAR = 3.0e38
PASSES = ((0, 0), (0, 1), (1, 0))


def wait(eng, sem, n):
    if isinstance(n, int) and n <= 0:
        return
    eng.wait_ge(sem, n)


def wait_alone(eng, sem, n, passed):
    wait(eng, sem, n)
    if not isinstance(n, int):
        eng.sem_inc(passed, 1)


class Tile:

    def __init__(self, b, j):
        self.batch = b + j // 2 if j // 2 else b
        self.par = j % 2

    def count(self, per=1, extra=0):
        return self.batch * (2 * per) + (self.par * per + per - extra)

    @property
    def index(self):
        return self.batch * 2 + self.par


def fold(nc, dram, keep, first):
    ctx = ExitStack()
    with ctx:
        sb = lambda n, s, d=F32: ctx.enter_context(nc.sbuf_tensor(n, s, d))
        pb = lambda n, s: ctx.enter_context(nc.psum_tensor(n, s, F32))
        sem = lambda n: ctx.enter_context(nc.semaphore(n))
        LOADS = 4
        LC = DC // LOADS
        GP = 4
        wo = sb("wo", [P, DC, D])
        wv = sb("wv", [P, HP, D])
        a_sb = sb("a_sb", [P, DC, R])
        woaT = sb("woaT", [R, D])
        woa = sb("woa", [P, HP, 2 * R])
        wvT = sb("wvT", [P, HP // GP, D])
        v_cols, a_cols = keep["v_cols"], keep["a_cols"]
        b_raw = sb("b_raw", [NF, R * P])
        b_hi, b_lo = sb("b_hi", [NF, R * P], F32R), sb("b_lo", [NF, R * P], F32R)
        mask8 = sb("mask8", [TS, B, M], U8)
        ps_woaT = pb("ps_woaT", [P, 2, 512])
        ps_woa = pb("ps_woa", [P, DC, R])
        ps_wvT = [pb(f"ps_wvT{i}", [P, 512]) for i in range(4)]
        ps_wv = [pb("ps_wv", [P, 512])[:], ps_woaT[:, 0], ps_woaT[:, 1]]
        ident_zero, ident_ready = sem("ident_zero"), sem("ident_ready")
        wo_in, wv_in = [sem(f"wo_in{i}") for i in range(LOADS)], [sem(f"wv_in{i}") for i in range(LOADS)]
        a_in, ln_in, b_in, mask_in = sem("a_in"), sem("ln_in"), sem("b_in"), sem("mask_in0")
        woaT_done, woaT_ready, woa_zero, woa_done, woa_ready, wvT_done, wvT_ready, wv_done, wv_evac, wvx_full = (
            sem(n) for n in ("woaT_done", "woaT_ready", "woa_zero", "woa_done", "woa_ready", "wvT_done", "wvT_ready",
                             "wv_done", "wv_evac", "wvx_full"))
        b_hi_ready, b_split, b_out, fold_done = (sem(n) for n in ("b_hi_ready", "b_split", "b_out", "fold_done"))
        block = ctx.enter_context(nc.Block())

        @block.sync
        def _(sp):
            sp.dma_start(a_sb[:], dram["a"].rearrange("(c p) r -> p c r", p=P)).then_inc(a_in, 16)
            sp.dma_start(b_raw[:], dram["b"]).then_inc(b_in, 16)
            for i in range(LOADS):
                sp.dma_start(wo[:, i * LC:(i + 1) * LC, :],
                             dram["wo"][i * LC * P:(i + 1) * LC * P, :].rearrange("(c p) n -> p c n", p=P)).then_inc(wo_in[i], 16)
            sp.wait_ge(b_split, 1)
            for i, part in enumerate((b_hi, b_lo, b_hi)):
                sp.dma_start(dram["b_stack"][:, i * R:(i + 1) * R].rearrange("f r n -> f (r n)"),
                             part[:].bitcast(F32)).then_inc(b_out, 16)
            sp.dma_start(keep["ln1"][:], dram["ln1"]).then_inc(ln_in, 16)
            sp.dma_start(keep["ln2"][:], dram["ln2"]).then_inc(ln_in, 16)
            sp.dma_start(mask8[:], dram["mask"].rearrange("(o b) m -> o b m", o=1).to_broadcast([TS, B, M])).then_inc(mask_in, 16)
            for i in range(LOADS):
                sp.dma_start(wv[:, i * LC:(i + 1) * LC, :],
                             dram["wv"][i * LC * P:(i + 1) * LC * P, :].rearrange("(c p) n -> p c n", p=P)).then_inc(wv_in[i], 16)
            for j in range(2):
                sp.dma_start(keep["xa"][:, j, :], dram["x"][j * TS:(j + 1) * TS, :]).then_inc(keep["xa_in"][j], 16)
            first.load(sp, chunks=range(first.RING))
            sp.wait_ge(b_out, 48)

        @block.gpsimd
        def _(pool):
            nc.gpsimd.memset(keep["ident"][:], 0.0).then_inc(ident_zero, 1)
            pool.wait_ge(ident_zero, 1)
            nc.gpsimd.affine_select(out=keep["ident"][:], in_=keep["ident"][:], compare_op=ALU.not_equal, fill=1.0,
                                    base=0, pattern=[[-1, P]], channel_multiplier=1).then_inc(ident_ready, 1)
            nc.gpsimd.memset(keep["causal"][:], 0.0).then_inc(ident_zero, 1)
            pool.wait_ge(ident_zero, 2)
            nc.gpsimd.affine_select(out=keep["causal"][:, TS:2 * TS], in_=keep["causal"][:, TS:2 * TS],
                                    compare_op=ALU.is_ge, fill=-FAR, base=0, pattern=[[-1, TS]],
                                    channel_multiplier=1).then_inc(ident_ready, 1)
            nc.gpsimd.memset(woa[:], 0.0).then_inc(woa_zero, 1)
            pool.wait_ge(b_hi_ready, 1)
            nc.gpsimd.tensor_tensor(b_lo[:], b_raw[:], b_hi[:].bitcast(F32), ALU.subtract).then_inc(b_split, 1)

        @block.tensor
        def _(pe):
            pe.wait_ge(a_in, 16)
            for co in range(DC):
                if co % LC == 0:
                    pe.wait_ge(wo_in[co // LC], 16)
                for h in range(2):
                    last = nc.tensor.matmul(ps_woaT[0:R, h, :], a_sb[:, co, :], wo[:, co, h * 512:(h + 1) * 512],
                                            start=(co == 0), stop=(co == DC - 1))
            last.then_inc(woaT_done, 1)
            pe.wait_ge(woaT_ready, 1)
            pe.wait_ge(ident_ready, 1)
            for ci in range(DC):
                last = nc.tensor.transpose(ps_woa[:, ci, :], woaT[:, ci * P:(ci + 1) * P], keep["ident"][0:R, 0:R])
            last.then_inc(woa_done, 1)
            pe.wait_ge(woa_ready, 2)
            for hp in range(HP):
                if hp % LC == 0:
                    pe.wait_ge(wv_in[hp // LC], 16)
                g = hp % GP
                for h in range(2):
                    last = nc.tensor.matmul(ps_wvT[hp // GP * 2 + h][g * 2 * R:(g + 1) * 2 * R, :], woa[:, hp, :],
                                            wv[:, hp, h * 512:(h + 1) * 512], start=True, stop=True)
                if g == GP - 1:
                    last.then_inc(wvT_done, 1)
            for g in range(HP // GP):
                pe.wait_ge(wvT_ready, 2 * g + 2)
                for q in range(2):
                    n = 2 * g + q
                    wait(pe, wv_evac, 4 * (n - 2))
                    for c in range(4 * q, 4 * q + 4):
                        last = nc.tensor.transpose(ps_wv[n % 3][:, c % 4 * P:(c % 4 + 1) * P], wvT[:, g, c * P:(c + 1) * P], keep["ident"][:])
                    last.then_inc(wv_done, 1)

        @block.scalar
        def _(act):
            act.wait_ge(b_in, 16)
            nc.scalar.activation(b_hi[:], b_raw[:], ACT.Copy).then_inc(b_hi_ready, 1)
            act.wait_ge(a_in, 16)
            act.wait_ge(ln_in, 32)
            for c in range(DC):
                nc.scalar.activation(a_cols[:, c], a_sb[:, c, :], ACT.Copy,
                                     scale=keep["ln2"][:, c:c + 1]).then_inc(wvx_full, 1)
            act.wait_ge(woaT_done, 1)
            nc.scalar.activation(woaT[:], ps_woaT[0:R].rearrange("p a n -> p (a n)"), ACT.Copy).then_inc(woaT_ready, 1)
            act.wait_ge(woa_zero, 1)
            act.wait_ge(woa_done, 1)
            nc.scalar.activation(woa[0:HD, :, 0:R], ps_woa[0:HD, :, :], ACT.Copy).then_inc(woa_ready, 1)
            nc.scalar.activation(woa[HD:P, :, R:2 * R], ps_woa[HD:P, :, :], ACT.Copy).then_inc(woa_ready, 1)
            for g in range(HP // GP):
                act.wait_ge(wvT_done, g + 1)
                for h in range(2):
                    nc.scalar.activation(wvT[:, g, h * 512:(h + 1) * 512], ps_wvT[2 * g + h][:], ACT.Copy).then_inc(wvT_ready, 1)

        @block.vector
        def _(dve):
            dve.wait_ge(mask_in, 16)
            nc.vector.tensor_reduce(keep["valid"][:], mask8[:], AX.X, ALU.max).then_inc(fold_done, 1)
            dve.wait_ge(ln_in, 32)
            for g in range(HP // GP):
                for q in range(2):
                    dve.wait_ge(wv_done, 2 * g + q + 1)
                    for c in range(4 * q, 4 * q + 4):
                        nc.vector.tensor_scalar(v_cols[:, c, g * P:(g + 1) * P], ps_wv[(2 * g + q) % 3][:, c % 4 * P:(c % 4 + 1) * P],
                                                keep["ln1"][:, c:c + 1], None, ALU.mult).then_inc(wv_evac, 1)


class Context:

    RING = 4

    def __init__(self, nc, dram, sb, sem):
        self.nc, self.dram = nc, dram
        self.raw = sb("ctT_raw", [P, self.RING, M])
        self.parts = sb("ctT", [P, DC, 2, MP], F32R)
        self.loaded = [sem(f"ctT_in{i}") for i in range(self.RING)]
        self.hi, self.lo, self.used = sem("ctT_hi"), sem("ctT_lo"), sem("ctT_used")

    def load(self, sp, b=0, passed=None, chunks=range(DC)):
        for c in chunks:
            wait_alone(sp, self.lo, b * DC + (c - self.RING + 1), passed)
            sp.dma_start(self.raw[:, c % self.RING, :],
                         self.dram["ctxT"][bass.ds(b, 1), c].rearrange("o p m -> p (o m)")).then_inc(self.loaded[c % self.RING], 16)

    def split_high(self, act, b=0, chunks=range(DC)):
        for c in chunks:
            wait(act, self.loaded[c % self.RING], (b * (DC // self.RING) + (c // self.RING + 1)) * 16)
            wait(act, self.used, b * (2 * DC) + (c + 1 - DC))
            self.nc.scalar.activation(self.parts[:, c, 0, 0:M], self.raw[:, c % self.RING, :], ACT.Copy).then_inc(self.hi, 1)

    def split_low(self, dve, b=0, chunks=range(DC)):
        for c in chunks:
            wait(dve, self.hi, b * DC + (c + 1))
            self.nc.vector.tensor_sub(self.parts[:, c, 1, 0:M], self.raw[:, c % self.RING, :],
                                      self.parts[:, c, 0, 0:M].bitcast(F32)).then_inc(self.lo, 1)


def cross(nc, dram, keep, first, weights):
    ctx = ExitStack()
    with ctx:
        sb = lambda n, s, d=F32: ctx.enter_context(nc.sbuf_tensor(n, s, d))
        pb = lambda n, s: ctx.enter_context(nc.psum_tensor(n, s, F32))
        sem = lambda n: ctx.enter_context(nc.semaphore(n))
        CXR = 3
        xa, xa_in = keep["xa"], keep["xa_in"]
        ctT, ctT_lo, ctT_used = first.parts, first.lo, first.used
        ctx_raw = sb("ctx_raw", [MS, CXR, D])
        cx = sb("cx", [MS, MC, 2, D], F32R)
        xb = sb("xb", [TS, 2, D])
        xn = sb("xn", [TS, D])
        xnT = sb("xnT", [P, 2, DC, TS], F32R)
        prob = sb("prob", [TS, 2, MP])
        pT = sb("pT", [MS, 2, MC, TS], F32R)
        z = sb("z", [TS, D])
        resid = sb("resid", [TS, D])
        zT = sb("zT", [P, 2, DC, TS], F32R)
        bias = sb("bias", [TS, MP])
        mask8 = sb("mask8b", [TS, M], U8)
        vout = sb("vout", [TS, H, 2, R], F32R)
        low = sb("low", [TS, 2])
        total = sb("total", [TS, 2])
        rinv = sb("rinv", [TS, 1])
        gain = sb("gain", [TS, 1])
        stats = sb("stats", [TS, 2, 6])
        x_stats = sb("x_stats", [TS, 2, 6])
        mv = sb("mv", [TS, 2])
        x_mv = sb("x_mv", [TS, 2])
        ve = sb("ve", [TS, 3])
        std = sb("std", [TS, 3])
        rstd = sb("rstd", [TS, 3])
        res_scale, res_bias = sb("res_scale", [TS, 1]), sb("res_bias", [TS, 1])
        ps_s = pb("ps_s", [P, 2, 512])
        ps_r = pb("ps_r", [P, 2, 512])
        ps_t = [pb("ps_t0", [P, 2, 512]), pb("ps_t1", [P, 2, 512])]

        cx_in = [sem(f"cx_in{i}") for i in range(CXR)]
        xb_in = [sem("xb_in0"), sem("xb_in1")]
        mask_in, pad_ready, bias_pad = sem("mask_in"), sem("pad_ready"), sem("bias_pad")
        wvx_hi, wvx_lo = sem("wvx_hi"), sem("wvx_lo")
        cx_hi, cx_lo, cx_used = (sem(n) for n in ("cx_hi", "cx_lo", "cx_used"))
        xn_ready, xT_done, xnT_hi, xnT_lo = (sem(n) for n in ("xn_ready", "xT_done", "xnT_hi", "xnT_lo"))
        bias_ready, low_ready, exp_done, pT_done, pT_hi, pT_lo = (sem(n) for n in ("bias_ready", "low_ready", "exp_done", "pT_done", "pT_hi", "pT_lo"))
        rinv_ready, gain_ready, x1_ready, st_ready, mv_ready, ve_half, ve_ready, std_ready, rstd_ready, ve_start, xst_ready, xmv_ready, xve_ready = (
            sem(n) for n in ("rinv_ready", "gain_ready", "x1_ready", "st_ready", "mv_ready", "ve_half", "ve_ready", "std_ready",
                             "rstd_ready", "ve_start", "xst_ready", "xmv_ready", "xve_ready"))
        z_ready, rsb_ready, resid_ready, resid_out = (sem(n) for n in ("z_ready", "rsb_ready", "resid_ready", "resid_out"))
        zT_done, zT_hi, zT_lo, zT_out, v_done, v_hi, v_lo, v_out, ha_ready = (
            sem(n) for n in ("zT_done", "zT_hi", "zT_lo", "zT_out", "v_done", "v_hi", "v_lo", "v_out", "ha_ready"))
        passed = {n: sem("passed_" + n) for n in ("sp", "pool", "dve")}
        block = ctx.enter_context(nc.Block())

        def schedule(eng, step):
            def run(b, j, steady):
                def at(k):
                    return Tile(b, j + k) if steady or 0 <= 2 * b + j + k < NT else None
                at.step = Tile(b, j)
                step(at)
            for t in range(-2, 4):
                run(t // 2, t % 2, False)
            with eng.Fori(2, B - 1) as b:
                run(b, 0, True)
                run(b, 1, True)
            for t in range(NT - 2, NT + 2):
                run(t // 2, t % 2, False)

        @block.sync
        def _(sp):
            def load_cx(b):
                for m in range(MC):
                    wait_alone(sp, cx_lo, b * MC + (m - CXR + 1), passed["sp"])
                    sp.dma_start(ctx_raw[:, m % CXR, :], dram["ctx"][bass.ds(b, 1), m].rearrange("o p d -> p (o d)")).then_inc(cx_in[m % CXR], 16)

            def load_xa(t):
                wait_alone(sp, xn_ready, t.count() - 2, passed["sp"])
                sp.dma_start(xa[:, t.par, :], dram["x"][bass.ds(t.index * TS, TS), :]).then_inc(xa_in[t.par], 16)

            def load_xb(t):
                wait(sp, resid_ready, t.count() - 2)
                wait_alone(sp, z_ready, t.count() - 2, passed["sp"])
                sp.dma_start(xb[:, t.par, :], dram["x"][bass.ds(t.index * TS, TS), :]).then_inc(xb_in[t.par], 16)

            def load_mask(b):
                wait_alone(sp, bias_ready, b, passed["sp"])
                sp.dma_start(mask8[:], dram["mask"][bass.ds(b, 1), :].to_broadcast([TS, M])).then_inc(mask_in, 16)

            def batch(b, last):
                if not last:
                    load_xa(Tile(b, 2))
                load_cx(b)
                load_xb(Tile(b, 0))
                if not last:
                    load_mask(b + 1)
                    load_xa(Tile(b, 3))
                    first.load(sp, b + 1, passed["sp"])
                load_xb(Tile(b, 1))

            load_mask(0)
            first.load(sp, chunks=range(first.RING, DC))
            batch(0, False)
            with sp.Fori(1, B - 1) as b:
                batch(b, False)
            batch(B - 1, True)
            wait(sp, wvx_lo, 2)
            weights.load(sp, 0, ("wk", "wq"), 0, None)

        @block.gpsimd
        def _(pool):
            nc.gpsimd.memset(ctT[:, :, :, M:MP].bitcast(F32), 0.0).then_inc(pad_ready, 1)
            nc.gpsimd.memset(bias[:, M:MP], -MASKED / CROSS_SCALE).then_inc(bias_pad, 1)

            def step(at):
                t, tm2 = at(1), at(-2)
                if t is not None and t.par == 0:
                    wait(pool, mask_in, (t.batch + 1) * 16)
                    wait(pool, bias_pad, 1)
                    wait_alone(pool, low_ready, t.batch * 2, passed["pool"])
                    nc.gpsimd.tensor_scalar(bias[:, 0:M], mask8[:], MASKED / CROSS_SCALE, -MASKED / CROSS_SCALE,
                                            ALU.mult, ALU.add).then_inc(bias_ready, 1)
                if t is None and tm2 is not None and at(-1) is None:
                    weights.scale(pool, 0, "ln1")
                if tm2 is not None:
                    wait(pool, resid_ready, tm2.count())
                    pool.dma_start(dram["resid"][bass.ds(tm2.index * TS, TS), :], resid[:]).then_inc(resid_out, 16)
                    wait(pool, zT_lo, tm2.count())
                    pool.dma_start(dram["zT"][:, bass.ds(tm2.index, 1)].rearrange("p o h c t -> p (o h) c t"),
                                   zT[:].bitcast(F32)).then_inc(zT_out, 16)
                    wait(pool, v_lo, tm2.count())
                    pool.dma_start(dram["v"][:, :, bass.ds(tm2.index, 1)].rearrange("q p o n -> p q (o n)"),
                                   vout[:].bitcast(F32).rearrange("p (q g) e r -> p q (g e r)", g=2)).then_inc(v_out, 16)
            schedule(pool, step)
            pool.wait_ge(resid_out, 16 * NT)
            pool.wait_ge(zT_out, 16 * NT)
            pool.wait_ge(v_out, 16 * NT)

        @block.tensor
        def _(pe):
            def step(at):
                t, t1, tm1, tm2 = at(0), at(1), at(-1), at(-2)

                def prob_transposed():
                    wait(pe, exp_done, tm1.count())
                    wait(pe, zT_lo, tm1.count() - 2)
                    for m in range(MC):
                        last = nc.tensor.transpose(ps_t[0][0:MS, m // 3, (m % 3) * TS:(m % 3 + 1) * TS],
                                                   prob[:, tm1.par, m * MS:(m + 1) * MS], keep["ident"][0:TS, 0:TS])
                    last.then_inc(pT_done, 1)

                if t is not None:
                    wait(pe, pad_ready, 1)
                    wait(pe, xnT_lo, t.count())
                    wait(pe, low_ready, t.count() - 1)
                    for c in range(DC):
                        if t.par == 0:
                            wait(pe, ctT_lo, t.batch * DC + (c + 1))
                        for m in range(2):
                            for i, (u, v) in enumerate(PASSES):
                                last = nc.tensor.matmul(ps_s[0:TS, m, 0:MH], xnT[:, u, c, :], ctT[:, c, v, m * MH:(m + 1) * MH],
                                                        start=(c == 0 and i == 0), stop=(c == DC - 1 and i == 2))
                        last.then_inc(ctT_used, 1)
                        if c == DC - 3 and tm1 is not None:
                            prob_transposed()
                elif tm1 is not None:
                    prob_transposed()
                if t1 is not None:
                    wait(pe, xn_ready, t1.count())
                    wait(pe, v_lo, t1.count() - 4)
                    wait(pe, ha_ready, t1.count() - 4)
                    for c in range(DC):
                        last = nc.tensor.transpose(ps_t[1][:, c // 4, (c % 4) * TS:(c % 4 + 1) * TS],
                                                   xn[:, c * P:(c + 1) * P], keep["ident"][0:TS, 0:TS])
                    last.then_inc(xT_done, 1)
                if tm2 is not None:
                    wait(pe, z_ready, tm2.count())
                    wait(pe, pT_lo, tm2.count() + 1 if tm1 is not None else NT)
                    for c in range(DC):
                        last = nc.tensor.transpose(ps_t[0][:, c // 4, (c % 4) * TS:(c % 4 + 1) * TS],
                                                   z[:, c * P:(c + 1) * P], keep["ident"][0:TS, 0:TS])
                    last.then_inc(zT_done, 1)
                if tm1 is not None:
                    wait(pe, pT_lo, tm1.count())
                    wait(pe, x1_ready, tm1.count() - 1)
                    for m in range(MC):
                        if tm1.par == 0:
                            wait(pe, cx_lo, tm1.batch * MC + (m + 1))
                        for h in range(2):
                            for i, (u, v) in enumerate(PASSES):
                                last = nc.tensor.matmul(ps_r[0:TS, h, :], pT[:, u, m, :], cx[:, m, v, h * 512:(h + 1) * 512],
                                                        start=(m == 0 and i == 0), stop=(m == MC - 1 and i == 2))
                        last.then_inc(cx_used, 1)
                if tm2 is not None:
                    wait(pe, wvx_lo, 2)
                    wait(pe, zT_lo, tm2.count())
                    wait(pe, xnT_lo, tm2.count() + 3 if t1 is not None else NT)
                    for c in range(DC):
                        for i, (u, v) in enumerate(PASSES):
                            last = nc.tensor.matmul(ps_t[1][0:TS, 0, 0:VW], zT[:, u, c, :], keep["wvx"][:, v, c, :],
                                                    start=(c == 0 and i == 0), stop=(c == DC - 1 and i == 2))
                    last.then_inc(v_done, 1)
            schedule(pe, step)

        T4 = lambda ps: ps[:, :, 0:4 * TS]
        W4 = lambda buf, u: buf[:, u].rearrange("p (a b) t -> p a (b t)", a=2)

        @block.scalar
        def _(act):
            def cx_high(b, ms):
                for m in ms:
                    wait(act, cx_in[m % CXR], (b * (MC // CXR) + (m // CXR + 1)) * 16)
                    wait(act, cx_used, b * (2 * MC) + (m + 1 - MC))
                    nc.scalar.activation(cx[:, m, 0, :], ctx_raw[:, m % CXR, :], ACT.Copy).then_inc(cx_hi, 1)

            def step(at):
                t, t1, tm1, tm2, tm3 = at(0), at(1), at(-1), at(-2), at(-3)
                odd = t is not None and t.par == 1
                start = t is None and t1 is not None
                if start:
                    first.split_high(act, 0, range(3))
                if odd:
                    cx_high(t.batch, (3, 4))
                if tm1 is not None:
                    wait(act, pT_done, tm1.count())
                    wait(act, cx_used, (tm1.count() - 1) * MC)
                    nc.scalar.activation(pT[:, 0].rearrange("p (a b) t -> p a (b t)", a=2),
                                         ps_t[0][0:MS, :, 0:3 * TS], ACT.Copy).then_inc(pT_hi, 1)
                if t1 is not None:
                    wait(act, xT_done, t1.count())
                    wait(act, ctT_used, (t1.count() - 1) * DC)
                    nc.scalar.activation(W4(xnT, 0), T4(ps_t[1]), ACT.Copy).then_inc(xnT_hi, 1)
                if start:
                    first.split_high(act, 0, range(3, DC))
                if odd:
                    cx_high(t.batch, (5,))
                if tm2 is not None:
                    wait(act, zT_done, tm2.count())
                    wait(act, v_done, tm2.count() - 1)
                    wait(act, zT_out, (tm2.count() - 1) * 16)
                    nc.scalar.activation(W4(zT, 0), T4(ps_t[0]), ACT.Copy).then_inc(zT_hi, 1)
                    wait(act, rsb_ready, tm2.count(2))
                    wait(act, resid_out, (tm2.count() - 1) * 16)
                    nc.scalar.activation(resid[:], xb[:, tm2.par, :], ACT.Identity, bias=res_bias[:],
                                         scale=res_scale[:]).then_inc(resid_ready, 1)
                if t is not None:
                    wait(act, low_ready, t.count())
                    wait(act, gain_ready, t.count() - 2)
                    nc.scalar.activation(prob[:, t.par, :], prob[:, t.par, :], ACT.Exp, bias=low[:, t.par:t.par + 1],
                                         scale=-1.0, accum_out=total[:, t.par:t.par + 1]).then_inc(exp_done, 1)
                    if t.par == 0:
                        cx_high(t.batch, (0, 1, 2))
                    elif at(1) is not None:
                        first.split_high(act, t.batch + 1)
                if tm1 is not None or at(2) is not None:
                    wait(act, ve_start, 1)
                    if tm1 is not None:
                        wait(act, ve_ready, tm1.count())
                    if at(2) is not None:
                        wait(act, xve_ready, at(2).count())
                    wait(act, rstd_ready, at.step.count(extra=-1))
                    nc.scalar.activation(std[:], ve[:], ACT.Sqrt).then_inc(std_ready, 1)
                if tm2 is not None:
                    wait(act, v_done, tm2.count())
                    wait(act, v_out, (tm2.count() - 1) * 16)
                    nc.scalar.activation(vout[:, :, 0, :], ps_t[1][0:TS, 0, 0:H * R].rearrange("p (h r) -> p h r", r=R),
                                         ACT.Copy).then_inc(v_hi, 1)
                    nc.scalar.activation(keep["ha"][:, bass.ds(tm2.index, 1), :].rearrange("p o r -> p (o r)"),
                                         ps_t[1][0:TS, 0, H * R:VW], ACT.Copy).then_inc(ha_ready, 1)
            schedule(act, step)

        @block.vector
        def _(dve):
            def cx_low(b, ms):
                for m in ms:
                    wait(dve, cx_hi, b * MC + (m + 1))
                    nc.vector.tensor_sub(cx[:, m, 1, :], ctx_raw[:, m % CXR, :], cx[:, m, 0, :].bitcast(F32)).then_inc(cx_lo, 1)

            def step(at):
                t, t1, t2, tm1, tm2 = at(0), at(1), at(2), at(-1), at(-2)
                if t1 is not None or tm2 is not None:
                    wait(dve, std_ready, at.step.count(extra=-1))
                    nc.vector.reciprocal(rstd[:], std[:]).then_inc(rstd_ready, 1)
                    wait(dve, rstd_ready, at.step.count(extra=-1))
                if tm2 is not None:
                    wait(dve, zT_done, tm2.count() - 1)
                    nc.vector.tensor_scalar(z[:], xb[:, tm2.par, :], mv[:, 0:1], rstd[:, 1:2], ALU.subtract, ALU.mult).then_inc(z_ready, 1)
                    wait(dve, resid_ready, tm2.count() - 1)
                    nc.vector.tensor_scalar(res_scale[:], rstd[:, 0:1], 1.0, None, ALU.add).then_inc(rsb_ready, 1)
                    nc.vector.tensor_scalar(res_bias[:], mv[:, 0:1], rstd[:, 0:1], -1.0, ALU.mult, ALU.mult).then_inc(rsb_ready, 1)
                if t1 is not None:
                    wait(dve, xT_done, t1.count() - 1)
                    nc.vector.tensor_scalar(xn[:], xa[:, t1.par, :], x_mv[:, 0:1], rstd[:, 2:3],
                                            ALU.subtract, ALU.mult).then_inc(xn_ready, 1)
                odd = t is not None and t.par == 1
                start = t is None and t1 is not None
                if start:
                    first.split_low(dve, 0, range(3))
                if odd:
                    cx_low(t.batch, (3, 4))
                if tm1 is not None:
                    wait(dve, pT_hi, tm1.count())
                    nc.vector.tensor_tensor(pT[:, 1].rearrange("p (a b) t -> p a (b t)", a=2), ps_t[0][0:MS, :, 0:3 * TS],
                                            pT[:, 0].rearrange("p (a b) t -> p a (b t)", a=2).bitcast(F32), ALU.subtract).then_inc(pT_lo, 1)
                if t1 is not None:
                    wait(dve, xnT_hi, t1.count())
                    nc.vector.tensor_tensor(W4(xnT, 1), T4(ps_t[1]), W4(xnT, 0).bitcast(F32), ALU.subtract).then_inc(xnT_lo, 1)
                if start:
                    first.split_low(dve, 0, range(3, DC))
                if odd:
                    cx_low(t.batch, (5,))
                if t is not None:
                    wait(dve, ctT_used, t.count() * DC)
                    wait(dve, bias_ready, t.batch + 1)
                    wait(dve, bias_pad, 1)
                    wait_alone(dve, pT_done, t.count() - 2, passed["dve"])
                    nc.vector.tensor_tensor_reduce(out=prob[:, t.par, :].rearrange("p (a m) -> p a m", a=2),
                                                   in0=ps_s[0:TS, :, 0:MH], in1=bias[:].rearrange("p (a m) -> p a m", a=2),
                                                   scale=-CROSS_SCALE, scalar=FAR, op0=ALU.add, op1=ALU.min,
                                                   accum_out=low[:, t.par:t.par + 1]).then_inc(low_ready, 1)
                if tm2 is not None:
                    wait(dve, zT_hi, tm2.count())
                    nc.vector.tensor_tensor(W4(zT, 1), T4(ps_t[0]), W4(zT, 0).bitcast(F32), ALU.subtract).then_inc(zT_lo, 1)
                if t2 is not None:
                    wait(dve, xa_in[t2.par], (t2.batch + 1) * 16)
                    for i in range(2):
                        nc.vector.bn_stats(x_stats[:, i, :], xa[:, t2.par, i * 512:(i + 1) * 512]).then_inc(xst_ready, 1)
                    wait(dve, xst_ready, t2.count(2))
                    wait_alone(dve, xn_ready, t2.count() - 1, passed["dve"])
                    nc.vector.bn_aggr(x_mv[:], x_stats[:]).then_inc(xmv_ready, 1)
                    wait(dve, xmv_ready, t2.count())
                    wait(dve, ve_start, 1)
                    nc.vector.tensor_scalar(ve[:, 2:3], x_mv[:, 1:2], LN_EPS, None, ALU.add).then_inc(xve_ready, 1)
                if odd and t1 is not None:
                    first.split_low(dve, t.batch + 1, range(DC // 2))
                if t is not None and t.par == 0:
                    cx_low(t.batch, (0, 1, 2))
                if t is not None and tm1 is None:
                    folded = ((slice(0, H * R), keep["v_cols"]), (slice(H * R, VW), keep["a_cols"][:]))
                    for cols, raw in folded:
                        nc.vector.tensor_copy(keep["wvx"][:, 0, :, cols], raw).then_inc(wvx_hi, 1)
                    wait(dve, wvx_hi, 2)
                    for cols, raw in folded:
                        nc.vector.tensor_sub(keep["wvx"][:, 1, :, cols], raw, keep["wvx"][:, 0, :, cols].bitcast(F32)).then_inc(wvx_lo, 1)
                if tm1 is not None:
                    wait(dve, exp_done, tm1.count())
                    nc.vector.reciprocal(rinv[:], total[:, tm1.par:tm1.par + 1]).then_inc(rinv_ready, 1)
                    wait(dve, rinv_ready, tm1.count())
                    nc.vector.tensor_scalar(gain[:], rinv[:], keep["valid"][:, bass.ds(tm1.batch, 1)], None, ALU.mult).then_inc(gain_ready, 1)
                    wait(dve, gain_ready, tm1.count())
                    wait(dve, xb_in[tm1.par], (tm1.batch + 1) * 16)
                    wait(dve, cx_used, tm1.count() * MC)
                    x1 = xb[:, tm1.par, :].rearrange("p (a n) -> p a n", a=2)
                    nc.vector.scalar_tensor_tensor(out=x1, in0=ps_r[0:TS], scalar=gain[:], in1=x1, op0=ALU.mult, op1=ALU.add).then_inc(x1_ready, 1)
                    wait(dve, x1_ready, tm1.count())
                    for i in range(2):
                        nc.vector.bn_stats(stats[:, i, :], xb[:, tm1.par, i * 512:(i + 1) * 512]).then_inc(st_ready, 1)
                    wait(dve, st_ready, tm1.count(2))
                    wait(dve, rsb_ready, tm1.count(2) - 2)
                    wait_alone(dve, z_ready, tm1.count() - 1, passed["dve"])
                    nc.vector.bn_aggr(mv[:], stats[:]).then_inc(mv_ready, 1)
                    wait(dve, mv_ready, tm1.count())
                    wait(dve, ve_start, 1)
                    nc.vector.tensor_scalar(ve[:, 0:1], mv[:, 1:2], LN_EPS, None, ALU.add).then_inc(ve_half, 1)
                    wait(dve, ve_half, tm1.count())
                    nc.vector.scalar_tensor_tensor(out=ve[:, 1:2], in0=ve[:, 0:1], scalar=RMS_EPS, in1=mv[:, 1:2],
                                                   op0=ALU.mult, op1=ALU.add).then_inc(ve_ready, 1)
                if odd and t1 is not None:
                    first.split_low(dve, t.batch + 1, range(DC // 2, DC))
                if tm2 is not None:
                    wait(dve, v_hi, tm2.count())
                    wait(dve, ha_ready, tm2.count())
                    nc.vector.tensor_tensor(vout[:, :, 1, :], ps_t[1][0:TS, 0, 0:H * R].rearrange("p (h r) -> p h r", r=R),
                                            vout[:, :, 0, :].bitcast(F32), ALU.subtract).then_inc(v_lo, 1)
            nc.vector.memset(ve[:], 1.0).then_inc(ve_start, 1)
            schedule(dve, step)


class Weights:

    def __init__(self, nc, dram, keep, sb, sem):
        self.nc, self.dram, self.keep = nc, dram, keep
        self.raw = sb("w_raw", [P, 2, DC, P])
        self.parts = None
        self.loaded = [sem("w_in0"), sem("w_in1")]
        self.scaled, self.hi, self.lo = sem("w_scaled"), sem("w_hi"), sem("w_lo")

    def load(self, sp, n, names, row, passed):
        for i, name in enumerate(names):
            wait_alone(sp, self.lo, n * 2 + (i - 1), passed)
            sp.dma_start(self.raw[:, i], self.dram[name][bass.ds(row, 1)].rearrange("o p c n -> p (o c) n")).then_inc(self.loaded[i], 16)

    def scale(self, pool, n, norm):
        for i in range(2):
            wait(pool, self.loaded[i], n * 16 + 16)
            self.nc.gpsimd.tensor_tensor(self.raw[:, i], self.raw[:, i], self.keep[norm][:].unsqueeze(2).to_broadcast([P, DC, P]),
                                         ALU.mult).then_inc(self.scaled, 1)

    def split_high(self, act, n, slot, i, use, used):
        wait(act, self.scaled, n * 2 + (i + 1))
        wait(act, use, used)
        self.nc.scalar.activation(self.parts[:, slot, i, 0], self.raw[:, i], ACT.Copy).then_inc(self.hi, 1)

    def split_low(self, dve, n, slot, i):
        wait(dve, self.hi, n * 2 + (i + 1))
        self.nc.vector.tensor_sub(self.parts[:, slot, i, 1], self.raw[:, i], self.parts[:, slot, i, 0].bitcast(F32)).then_inc(self.lo, 1)


def self_attention(nc, dram, keep, weights, zz):
    ctx = ExitStack()
    with ctx:
        sb = lambda n, s, d=F32: ctx.enter_context(nc.sbuf_tensor(n, s, d))
        pb = lambda n, s: ctx.enter_context(nc.psum_tensor(n, s, F32))
        sem = lambda n: ctx.enter_context(nc.semaphore(n))
        UNITS = 4
        STEPS = HP * NB
        w, w_lo = weights.parts, weights.lo
        q_stack = sb("q_stack", [P, 2, 2, BW], F32R)
        k_high = sb("k_high", [P, 2, 2, BW], F32R)
        k_low = sb("k_low", [P, 2, BW], F32R)
        high_rows = [slice(HD, P), slice(0, HD)]
        low_rows = [slice(0, HD), slice(HD, P)]
        vb = sb("vb", [TS, 2, NT, 2, 2 * R], F32R)
        prob = sb("prob2", [TS, UNITS, 3 * TS])
        keys_of = lambda qt: slice(qt * TS, (2 * qt + 1) * TS)
        probT = sb("probT", [TS, 2, 2, 4, TS], F32R)
        acc_all = sb("acc", [P, T])
        acc = acc_all[0:2 * R]
        low = sb("low2", [TS, UNITS, 2])
        total = sb("total2", [TS, UNITS, 2])
        rinv = sb("rinv2", [TS, UNITS, 2])
        spare = prob[:].rearrange("p u k -> p (u k)")
        tiles = lambda at, n: spare[:, at * NT:(at + n) * NT].rearrange("p (t n) -> p t n", n=n)
        sums, mod, u, u_hi = tiles(0, 2 * R), tiles(2 * R, R), tiles(3 * R, R), tiles(4 * R, R).bitcast(F32R)
        u3 = acc_all[0:TS, 0:NT * 3 * R].rearrange("p (t n) -> p t n", n=3 * R)
        uT = keep["uT"]
        ps_p = [pb("ps_k", [P, 512]), pb("ps_q", [P, 512])]
        ps_s = [pb("ps_s0", [P, 512]), pb("ps_s1", [P, 512])]
        ps_t = [pb("ps_pt0", [P, 512]), pb("ps_pt1", [P, 512])]
        ps_o = [pb("ps_o0", [P, 512]), pb("ps_o1", [P, 512])]
        zz_in = [sem(f"zz_in{i}") for i in range(NB)]
        z0_in = [sem(f"z0_in{i}") for i in range(DC // 2)]
        vb_in = [sem("vb_in0"), sem("vb_in1")]
        proj_done, qk_hi, qk_lo = (sem(n) for n in ("proj_done", "qk_hi", "qk_lo"))
        s_done, low_ready, exp_done, rinv_ready, prob_ready = (sem(n) for n in ("s_done", "low_ready2", "exp_done2", "rinv_ready2", "prob_ready"))
        pt_done, pt_hi, pt_lo, pv_done, o_added, zeroed, acc_zero = (sem(n) for n in ("pt_done", "pt_hi", "pt_lo", "pv_done", "o_added", "zeroed", "acc_zero"))
        sums_done, sums_ready, attn_ready, mod_ready, u_ready, u3_part, u3_ready, uT_done, uT_ready = (
            sem(n) for n in ("sums_done", "sums_ready", "attn_ready", "mod_ready", "u_ready", "u3_part", "u3_ready", "uT_done", "uT_ready"))
        passed = {n: sem("passed_" + n) for n in ("sp", "pool", "dve")}
        block = ctx.enter_context(nc.Block())

        class Unit:

            def __init__(self, pair, x):
                self.pair = pair + x // 16 if x // 16 else pair
                self.x = x % 16
                self.blk, self.u = self.x // UNITS, self.x % UNITS
                self.bi, self.head = self.u // 2, self.u % 2
                self.spar = self.blk % 2

            @property
            def count(self):
                return self.pair * 16 + (self.x + 1)

            def step(self, off=0):
                return self.pair * NB + (self.blk + off)

        def schedule(eng, quarter):
            def run(pair, ppar, x, steady):
                def at(k):
                    n = x + k
                    if not (steady or 0 <= 16 * pair + n < 16 * HP):
                        return None, 0
                    return Unit(pair, n), (ppar + n // 16) % 2
                quarter(pair if steady or pair < HP else None, ppar, x, at)
            for x in range(16):
                run(0, 0, x, False)
            for x in range(16):
                run(1, 1, x, True)
            with eng.Fori(2, HP - 1, 2) as pair:
                for x in range(16):
                    run(pair, 0, x, True)
                for x in range(16):
                    run(pair + 1, 1, x, True)
            for x in range(UNITS + 3):
                run(HP, 0, x, False)

        HIGH, LOW = 6, 4

        SC, PT, PV = -UNITS, -UNITS - 2, -UNITS - 3

        @block.sync
        def _(sp):
            def load_w(pair):
                weights.load(sp, pair, ("wk", "wq"), pair, passed["sp"])

            def load_v(pair, ppar):
                wait_alone(sp, pv_done, (pair - 1) * 16, passed["sp"])
                sp.dma_start(vb[:, ppar].bitcast(F32).rearrange("p t g n -> p t (g n)"),
                             dram["v"][bass.ds(pair, 1)].rearrange("o p t n -> p (o t) n")).then_inc(vb_in[ppar], 16)

            for i in range(DC // 2):
                sp.dma_start(zz[0][:, 0:BT, :, 2 * i:2 * i + 2].bitcast(F32),
                             dram["zT"][:, 0:BT, :, 2 * i:2 * i + 2]).then_inc(z0_in[i], 16)
            for i in range(1, NB):
                if i == NB - 1:
                    load_w(1)
                    load_v(0, 0)
                sp.dma_start(zz[i // 2][:, i % 2 * BT:(i % 2 + 1) * BT].bitcast(F32), dram["zT"][:, i * BT:(i + 1) * BT]).then_inc(zz_in[i], 16)
            load_v(1, 1)
            with sp.Fori(2, HP - 1, 2) as pair:
                load_w(pair)
                load_v(pair, 0)
                load_w(pair + 1)
                load_v(pair + 1, 1)
            weights.load(sp, HP, ("w_in", "w_up"), 0, passed["sp"])

        @block.tensor
        def _(pe):
            def quarter(pair, ppar, x, at):
                blk, q = x // 4, x % 4
                if pair is not None:
                    i, half = q // 2, q % 2
                    if half == 0:
                        if isinstance(pair, int) and pair == 0 and blk:
                            wait(pe, zz_in[blk], 16)
                        if blk == 0:
                            wait(pe, w_lo, pair * 2 + (i + 1))
                        wait(pe, qk_hi, pair * (HIGH * NB) + (HIGH * (blk - 1) + (HIGH if i else 4)))
                        wait(pe, qk_lo, pair * (LOW * NB) + (LOW * (blk - 1) + 2 * (i + 1)))
                    for c in range(half * DC // 2, (half + 1) * DC // 2):
                        if isinstance(pair, int) and pair == 0 and x < 2 and c % 2 == 0:
                            wait(pe, z0_in[c // 2], 16)
                        for n, (a, b) in enumerate(PASSES):
                            last = nc.tensor.matmul(ps_p[i][:, 0:BW], w[:, ppar, i, a, c, :], zz[blk // 2][:, blk % 2 * BT:(blk % 2 + 1) * BT, b, c, :],
                                                    start=(c == 0 and n == 0), stop=(c == DC - 1 and n == 2))
                    if half:
                        last.then_inc(proj_done, 1)
                s, _ = at(SC)
                if s is not None:
                    if s.u == 0:
                        wait(pe, qk_lo, s.step(1) * LOW)
                    wait(pe, low_ready, (s.count - 2) * 2)
                    queries = q_stack[:, s.spar, s.head, s.bi * S:(s.bi + 1) * S]
                    keys, rows = slice(s.bi * S, (s.bi + 1) * S), high_rows[s.head]
                    for qt in range(2):
                        nc.tensor.matmul(ps_s[s.u % 2][0:TS, qt * S:(qt + 1) * S], queries[:, qt * TS:(qt + 1) * TS],
                                         k_high[:, s.spar, s.head, keys], start=True, stop=False)
                        last = nc.tensor.matmul(ps_s[s.u % 2][0:TS, qt * S:(qt + 1) * S], queries[rows, qt * TS:(qt + 1) * TS],
                                                k_low[rows, s.spar, keys], start=False, stop=True)
                    last.then_inc(s_done, 1)
                t, _ = at(PT)
                if t is not None:
                    wait(pe, prob_ready, t.count * 2)
                    wait(pe, pt_lo, t.count - 2)
                    for n, (qt, kt) in enumerate(((0, 0), (1, 0), (1, 1))):
                        last = nc.tensor.transpose(ps_t[t.u % 2][0:TS, n * TS:(n + 1) * TS],
                                                   prob[:, t.u, (qt + kt) * TS:(qt + kt + 1) * TS], keep["ident"][0:TS, 0:TS])
                    last.then_inc(pt_done, 1)
                v, vpar = at(PV)
                if v is not None:
                    wait(pe, pt_lo, v.count)
                    if v.x == 0:
                        wait(pe, vb_in[vpar], (v.pair - vpar) * 8 + 16)
                    if v.head == 0:
                        wait(pe, o_added, v.pair * 8 + (v.x // 2 - 1))
                    for n, (kt, b) in enumerate(((0, 0), (1, 0), (0, 1), (1, 1))):
                        last = nc.tensor.matmul(ps_o[v.bi][0:2 * R, 0:S],
                                                vb[:, vpar, v.blk * BT + v.bi * 2 + kt, v.head, :],
                                                probT[:, v.u % 2, b, (1 - kt):(3 if kt == 0 else 4):(1 if kt == 0 else 3), :],
                                                start=(v.head == 0 and n == 0), stop=(v.head == 1 and n == 3))
                    last.then_inc(pv_done, 1)
            schedule(pe, quarter)
            pe.wait_ge(o_added, 8 * HP)
            for t in range(NT):
                last = nc.tensor.transpose(ps_s[0][0:TS, t * 2 * R:(t + 1) * 2 * R], acc[:, t * TS:(t + 1) * TS],
                                           keep["ident"][0:2 * R, 0:2 * R])
            last.then_inc(sums_done, 1)
            pe.wait_ge(u3_ready, 3)
            for t in range(NT):
                if t % BT == 0:
                    wait(pe, uT_ready, t // BT - 1)
                last = nc.tensor.transpose(ps_p[t // BT % 2][0:3 * R, t % BT * TS:(t % BT + 1) * TS], u3[:, t, :],
                                           keep["ident"][0:TS, 0:TS])
                if t % BT == BT - 1:
                    last.then_inc(uT_done, 1)

        @block.scalar
        def _(act):
            def split_high(pair, ppar, i):
                weights.split_high(act, pair, ppar, i, proj_done, (pair - 1) * (2 * NB))

            def quarter(pair, ppar, x, at):
                blk, q = x // 4, x % 4
                if pair is not None and q % 2 == 1:
                    i = q // 2
                    wait(act, proj_done, pair * (2 * NB) + (2 * blk + i + 1))
                    wait(act, s_done, pair * 16 + (blk - 1) * 4)
                    for h in range(2):
                        rows = ps_p[i][h * HD:(h + 1) * HD, 0:BW]
                        for to in (high_rows[h:h + 1] if i else low_rows):
                            nc.scalar.activation((q_stack if i else k_high)[to, blk % 2, h], rows, ACT.Copy).then_inc(qk_hi, 1)
                t, _ = at(PT)
                if t is not None:
                    wait(act, pt_done, t.count)
                    wait(act, zeroed, 2)
                    wait(act, pv_done, t.count - 2)
                    nc.scalar.activation(probT[:, t.u % 2, 0, 1:4, :].rearrange("p b t -> p (b t)"),
                                         ps_t[t.u % 2][0:TS, 0:3 * TS], ACT.Copy).then_inc(pt_hi, 1)
                s, _ = at(SC)
                if s is not None:
                    wait(act, rinv_ready, s.count - UNITS)
                    for qt in range(2):
                        wait(act, low_ready, (s.count - 1) * 2 + (qt + 1))
                        nc.scalar.activation(prob[:, s.u, keys_of(qt)], prob[:, s.u, keys_of(qt)], ACT.Exp,
                                             bias=low[:, s.u, qt:qt + 1], scale=-1.0,
                                             accum_out=total[:, s.u, qt:qt + 1]).then_inc(exp_done, 1)
                if pair is not None and x in (4, 6):
                    split_high(pair + 1, 1 - ppar, (x - 4) // 2)

            split_high(0, 0, 0)
            split_high(0, 0, 1)
            schedule(act, quarter)
            act.wait_ge(attn_ready, 1)
            nc.scalar.activation(mod, mod, ACT.Tanh).then_inc(mod_ready, 1)
            for i in range(NB):
                act.wait_ge(uT_done, i + 1)
                nc.scalar.activation(uT[:, i * BW:(i + 1) * BW], ps_p[i % 2][0:3 * R, 0:BW], ACT.Copy).then_inc(uT_ready, 1)

        @block.gpsimd
        def _(pool):
            nc.gpsimd.memset(probT[:, 0, :, 0, :].bitcast(F32), 0.0).then_inc(zeroed, 1)
            nc.gpsimd.memset(probT[:, 1, :, 0, :].bitcast(F32), 0.0).then_inc(zeroed, 1)

            with pool.Fori(1, HP) as pair:
                weights.scale(pool, pair, "ln1")
            weights.scale(pool, HP, "ln2")

        @block.vector
        def _(dve):
            def split_low(pair, ppar, i):
                weights.split_low(dve, pair, ppar, i)

            def quarter(pair, ppar, x, at):
                blk, q = x // 4, x % 4
                if pair is not None and q % 2 == 1:
                    i = q // 2
                    for h in range(2):
                        wait(dve, qk_hi, pair * (HIGH * NB) + (HIGH * blk + (4 + h + 1 if i else 2 * (h + 1))))
                        high, out = (q_stack, q_stack[low_rows[h], blk % 2, h]) if i else (k_high, k_low[high_rows[h], blk % 2])
                        nc.vector.tensor_tensor(out, ps_p[i][h * HD:(h + 1) * HD, 0:BW],
                                                high[high_rows[h], blk % 2, h].bitcast(F32), ALU.subtract).then_inc(qk_lo, 1)
                s, _ = at(SC)
                if s is not None:
                    wait(dve, s_done, s.count)
                    wait(dve, acc_zero, 1)
                    wait_alone(dve, pt_done, s.count - UNITS, passed["dve"])
                    for qt in range(2):
                        kw = (qt + 1) * TS
                        nc.vector.tensor_tensor_reduce(out=prob[:, s.u, keys_of(qt)], in0=ps_s[s.u % 2][0:TS, qt * S:qt * S + kw],
                                                       in1=keep["causal"][:, S - kw:S], scale=-SELF_SCALE, scalar=FAR,
                                                       op0=ALU.add, op1=ALU.min,
                                                       accum_out=low[:, s.u, qt:qt + 1]).then_inc(low_ready, 1)
                t, _ = at(PT)
                if t is not None:
                    wait(dve, pt_hi, t.count)
                    nc.vector.tensor_tensor(probT[:, t.u % 2, 1, 1:4, :].rearrange("p b t -> p (b t)"),
                                            ps_t[t.u % 2][0:TS, 0:3 * TS],
                                            probT[:, t.u % 2, 0, 1:4, :].rearrange("p b t -> p (b t)").bitcast(F32),
                                            ALU.subtract).then_inc(pt_lo, 1)
                v, _ = at(PV)
                if v is not None and v.head == 1:
                    wait(dve, pv_done, v.count)
                    wait(dve, acc_zero, 1)
                    cols = slice((v.blk * BT + v.bi * 2) * TS, (v.blk * BT + v.bi * 2 + 2) * TS)
                    nc.vector.tensor_tensor(acc[:, cols], ps_o[v.bi][0:2 * R, 0:S], acc[:, cols], ALU.add).then_inc(o_added, 1)
                if s is not None:
                    wait(dve, exp_done, s.count * 2)
                    nc.vector.reciprocal(rinv[:, s.u], total[:, s.u]).then_inc(rinv_ready, 1)
                    wait(dve, rinv_ready, s.count)
                    for qt in range(2):
                        nc.vector.tensor_scalar(prob[:, s.u, keys_of(qt)], prob[:, s.u, keys_of(qt)], rinv[:, s.u, qt:qt + 1],
                                                None, ALU.mult).then_inc(prob_ready, 1)
                if pair is not None and x in (4, 6):
                    split_low(pair + 1, 1 - ppar, (x - 4) // 2)

            split_low(0, 0, 0)
            split_low(0, 0, 1)
            nc.vector.memset(acc[:], 0.0).then_inc(acc_zero, 1)
            schedule(dve, quarter)
            dve.wait_ge(sums_done, 1)
            nc.vector.tensor_copy(spare[:, 0:2 * R * NT], ps_s[0][0:TS, :]).then_inc(sums_ready, 1)
            dve.wait_ge(sums_ready, 1)
            nc.vector.tensor_tensor(mod, sums[:, :, 0:R], sums[:, :, R:2 * R], ALU.add).then_inc(attn_ready, 1)
            dve.wait_ge(mod_ready, 1)
            nc.vector.scalar_tensor_tensor(out=u, in0=mod, scalar=MOD_SCALE, in1=keep["ha"][:], op0=ALU.mult,
                                           op1=ALU.mult).then_inc(u_ready, 1)
            dve.wait_ge(u_ready, 1)
            nc.vector.tensor_copy(u_hi, u).then_inc(u3_part, 1)
            dve.wait_ge(u3_part, 1)
            for i in range(2):
                nc.vector.tensor_copy(u3[:, :, i * R:(i + 1) * R], u_hi.bitcast(F32)).then_inc(u3_ready, 1)
            nc.vector.tensor_sub(u3[:, :, 2 * R:3 * R], u, u_hi.bitcast(F32)).then_inc(u3_ready, 1)


def ffn(nc, dram, keep, weights, zh):
    ctx = ExitStack()
    with ctx:
        sb = lambda n, s, d=F32: ctx.enter_context(nc.sbuf_tensor(n, s, d))
        pb = lambda n, s: ctx.enter_context(nc.psum_tensor(n, s, F32))
        sem = lambda n: ctx.enter_context(nc.semaphore(n))
        HT = T // 2
        BLK = HT // BW
        JT = HT // P
        G = 4
        gu, gu_lo = weights.parts, weights.lo
        wd_raw = sb("wd_raw", [P, D])
        wd = sb("wd", [P, G, 2, D], F32R)
        bs = sb("bs", [3 * R, 2, P], F32R)
        uT = keep["uT"]
        gate = sb("gate", [P, 2, BW])
        prod = sb("prod", [P, 2, BW])
        hid = sb("hid", [P, G, 2, HT], F32R)
        acc = sb("out_acc", [P, JT, D])
        ps_g = [pb("ps_g0", [P, 512]), pb("ps_g1", [P, 512])]
        ps_u = [pb("ps_u0", [P, 512]), pb("ps_u1", [P, 512])]
        ps_d = [pb(f"ps_d{i}", [P, 512]) for i in range(4)]
        zh_in = [sem("zh_in0"), sem("zh_in1")]
        acc_in = sem("acc_in")
        wd_in = sem("wd_in")
        bs_in = [sem("bs_in0"), sem("bs_in1")]
        wd_hi, wd_lo = sem("wd_hi"), sem("wd_lo")
        gate_done, up_done, silu_ready, prod_ready, hid_hi, hid_lo, down_done, added, out_done = (
            sem(n) for n in ("gate_done", "up_done", "silu_ready", "prod_ready", "hid_hi", "hid_lo", "down_done", "added", "out_done"))
        ADDS = JT * 2
        passed = {n: sem("passed_" + n) for n in ("sp", "pool", "dve")}
        block = ctx.enter_context(nc.Block())

        def schedule(eng, step, down):
            def turn(base, half, first):
                for k in range(G):
                    step(base + k, k, half)
                    if k % 2 == 0 and not (first and k == 0):
                        down(base + (k - 2), (k - 2) % G, half)
            for half in range(2):
                turn(half * NF, half, True)
                with eng.Fori(half * NF + G, (half + 1) * NF - G + 1, G) as base:
                    turn(base, half, False)
                down((half + 1) * NF - 2, G - 2, half)

        @block.sync
        def _(sp):
            def load(n, f, k):
                if not (isinstance(n, int) and n == 0):
                    weights.load(sp, n + HP, ("w_in", "w_up"), f, passed["sp"])
                wait_alone(sp, gate_done, (n - 1) * BLK, passed["sp"])
                sp.dma_start(bs[:, k % 2].bitcast(F32), dram["b_stack"][bass.ds(f, 1)].rearrange("o k n -> (o k) n")).then_inc(bs_in[k % 2], 16)
                wait_alone(sp, wd_lo, n, passed["sp"])
                sp.dma_start(wd_raw[:], dram["w_down"][bass.ds(f, 1)].rearrange("o p d -> (o p) d")).then_inc(wd_in, 16)

            for half in range(2):
                rows = slice(half * HT, (half + 1) * HT)
                load(half * NF, 0, 0)
                if half:
                    sp.wait_ge(up_done, NF * BLK)
                    for i in range(BLK):
                        sp.dma_start(zh[:, i * BT:(i + 1) * BT].bitcast(F32),
                                     dram["zT"][:, (BLK + i) * BT:(BLK + i + 1) * BT]).then_inc(zh_in[i], 16)
                load(half * NF + 1, 1, 1)
                if half:
                    sp.wait_ge(added, NF // 2 * ADDS)
                    sp.dma_start(dram["out"][0:HT, :].rearrange("(j p) d -> p j d", p=P), acc[:]).then_inc(out_done, 16)
                    sp.wait_ge(out_done, 16)
                sp.dma_start(acc[:], dram["resid"][rows, :].rearrange("(j p) d -> p j d", p=P)).then_inc(acc_in, 16)
                for k in range(2, G):
                    load(half * NF + k, k, k)
                with sp.Fori(G, NF - G + 1, G) as f:
                    for k in range(G):
                        load(f + (half * NF + k), f + k, k)
            load(2 * NF, 0, 0)
            for j in range(JT):
                sp.wait_ge(added, (NF - 1) * ADDS + 2 * (j + 1))
                sp.dma_start(dram["out"][HT + j * P:HT + (j + 1) * P, :], acc[:, j]).then_inc(out_done, 16)
            sp.wait_ge(out_done, 16 * (JT + 1))

        @block.gpsimd
        def _(pool):
            with pool.Fori(1, 2 * NF + 1) as n:
                weights.scale(pool, n + HP, "ln2")

        @block.tensor
        def _(pe):
            def step(n, k, half):
                wait(pe, gu_lo, n * 2 + (2 * HP + 2))
                wait(pe, bs_in[k % 2], n * 8 + (2 - k % 2) * 8)
                for b in range(BLK):
                    if k == 0 and half:
                        wait(pe, zh_in[b], 16)
                    z = lambda part, c: zh[:, b * BT:(b + 1) * BT, part, c, :]
                    wait(pe, silu_ready, n * BLK + (b - 1))
                    for c in range(DC):
                        for i, (u, v) in enumerate(PASSES):
                            nc.tensor.matmul(ps_g[b][:, 0:BW], gu[:, k % 2, 0, u, c, :], z(v, c), start=(c == 0 and i == 0), stop=False)
                    nc.tensor.matmul(ps_g[b][:, 0:BW], bs[:, k % 2, :], uT[:, half * HT + b * BW:half * HT + (b + 1) * BW], start=False, stop=True).then_inc(gate_done, 1)
                    wait(pe, prod_ready, n * BLK + (b - 1))
                    for c in range(DC):
                        for i, (u, v) in enumerate(PASSES):
                            last = nc.tensor.matmul(ps_u[b][:, 0:BW], gu[:, k % 2, 1, u, c, :], z(v, c),
                                                    start=(c == 0 and i == 0), stop=(c == DC - 1 and i == 2))
                    last.then_inc(up_done, 1)

            def down(n, k, half):
                wait(pe, wd_lo, n + 2)
                wait(pe, hid_lo, n * BLK + 2 * BLK)
                for at in range(ADDS):
                    j, h = at // 2, at % 2
                    wait(pe, added, n * JT + (at - 3))
                    for g in range(2):
                        for i, (u, v) in enumerate(PASSES):
                            last = nc.tensor.matmul(ps_d[(k // 2 * ADDS + at) % 4][:], hid[:, k + g, u, j * P:(j + 1) * P],
                                                    wd[:, k + g, v, h * 512:(h + 1) * 512],
                                                    start=(g == 0 and i == 0), stop=(g == 1 and i == 2))
                    last.then_inc(down_done, 1)
            schedule(pe, step, down)

        @block.scalar
        def _(act):
            def split(n, k):
                for i in range(2):
                    weights.split_high(act, n + HP, k % 2, i, up_done if i else gate_done, (n - 1) * BLK)

            def split_down(n, k):
                wait(act, wd_in, n * 16 + 16)
                wait(act, down_done, n * JT - (k % 2 + 2) * JT)
                nc.scalar.activation(wd[:, k, 0], wd_raw[:], ACT.Copy).then_inc(wd_hi, 1)

            def step(n, k, half):
                split(n + 1, (k + 1) % G)
                for b in range(BLK):
                    wait(act, gate_done, n * BLK + (b + 1))
                    wait(act, prod_ready, n * BLK + (b - 1))
                    nc.scalar.activation(gate[:, b], ps_g[b][:, 0:BW], ACT.Silu).then_inc(silu_ready, 1)
                    if b == 0:
                        split_down(n + 1, (k + 1) % G)
                    wait(act, prod_ready, n * BLK + (b + 1))
                    wait(act, down_done, n * JT - (k % 2 + 2) * JT)
                    nc.scalar.activation(hid[:, k, 0, b * BW:(b + 1) * BW], prod[:, b], ACT.Copy).then_inc(hid_hi, 1)
            split_down(0, 0)
            schedule(act, step, lambda *a: None)

        @block.vector
        def _(dve):
            def split(n, k):
                for i in range(2):
                    weights.split_low(dve, n + HP, k % 2, i)

            def split_down(n, k):
                wait(dve, wd_hi, n + 1)
                nc.vector.tensor_sub(wd[:, k, 1], wd_raw[:], wd[:, k, 0].bitcast(F32)).then_inc(wd_lo, 1)

            def step(n, k, half):
                split(n + 1, (k + 1) % G)
                for b in range(BLK):
                    wait(dve, up_done, n * BLK + (b + 1))
                    wait(dve, silu_ready, n * BLK + (b + 1))
                    wait(dve, hid_lo, n * BLK + (b - 1))
                    nc.vector.tensor_tensor(prod[:, b], gate[:, b], ps_u[b][:, 0:BW], ALU.mult).then_inc(prod_ready, 1)
                    if b == 0:
                        split_down(n + 1, (k + 1) % G)
                    wait(dve, hid_hi, n * BLK + (b + 1))
                    nc.vector.tensor_sub(hid[:, k, 1, b * BW:(b + 1) * BW], prod[:, b],
                                         hid[:, k, 0, b * BW:(b + 1) * BW].bitcast(F32)).then_inc(hid_lo, 1)

            def down(n, k, half):
                dve.wait_ge(acc_in, (half + 1) * 16)
                for at in range(ADDS):
                    j, h = at // 2, at % 2
                    wait(dve, down_done, n * JT + (at + 1))
                    part = acc[:, j, h * 512:(h + 1) * 512]
                    nc.vector.tensor_tensor(part, ps_d[(k // 2 * ADDS + at) % 4][:], part, ALU.add).then_inc(added, 1)
            split_down(0, 0)
            schedule(dve, step, down)


def program(nc, dram):
    ctx = ExitStack()
    with ctx:
        sb = lambda n, s, d=F32: ctx.enter_context(nc.sbuf_tensor(n, s, d))
        dr = lambda n, s, d=F32: nc.dram_tensor(n, s, d, kind="Internal").ap()
        dram = dict(dram)
        dram["zT"] = dr("zT_dram", (P, NT, 2, DC, TS))
        dram["v"] = dr("v_dram", (HP, TS, NT, 4 * R))
        dram["resid"] = dr("resid_dram", (T, D))
        dram["b_stack"] = dr("b_stack_dram", (NF, 3 * R, P))
        sem = lambda n: ctx.enter_context(nc.semaphore(n))
        keep = {
            "ident": sb("ident", [P, P]),
            "causal": sb("causal", [TS, S]),
            "ln1": sb("ln1", [P, DC]),
            "ln2": sb("ln2", [P, DC]),
            "ha": sb("ha", [TS, NT, R]),
        }
        weights = Weights(nc, dram, keep, sb, sem)
        with ExitStack() as inner:
            isb = lambda n, s, d=F32: inner.enter_context(nc.sbuf_tensor(n, s, d))
            keep["wvx"] = isb("keep_wvx", [P, 2, DC, VW], F32R)
            keep["v_cols"] = weights.raw[:].rearrange("p i c n -> p (i c n)").rearrange("p (c n) -> p c n", c=DC)
            keep["a_cols"] = isb("a_cols", [P, DC, R])
            keep["valid"] = isb("valid", [TS, B])
            keep["xa"] = isb("xa", [TS, 2, D])
            keep["xa_in"] = [inner.enter_context(nc.semaphore(f"xa_in{i}")) for i in range(2)]
            first = Context(nc, dram, isb, lambda n: inner.enter_context(nc.semaphore(n)))
            fold(nc, dram, keep, first)
            cross(nc, dram, keep, first, weights)
        weights.parts = sb("w", [P, 2, 2, 2, DC, P], F32R)
        keep["uT"] = sb("uT", [3 * R, T], F32R)
        z_first = sb("z_first", [P, NT // 2, 2, DC, TS], F32R)
        with nc.sbuf_tensor("z_last", [P, NT // 2, 2, DC, TS], F32R) as z_last:
            self_attention(nc, dram, keep, weights, (z_first, z_last))
        ffn(nc, dram, keep, weights, z_first)


def kernel(**inputs):
    import numpy as np
    import concourse.bacc as bacc
    from concourse.bass_utils import run_bass_kernel_spmd

    a = {k: np.asarray(v) for k, v in inputs.items()}
    columns = lambda w, n: w.reshape(n, P, DC, P).transpose(0, 3, 2, 1)
    laid = {
        "x": a["x"].reshape(T, D),
        "ctx": a["ctx_2048"].reshape(B, MC, MS, D),
        "ctxT": a["ctx_2048"].transpose(0, 2, 1).reshape(B, DC, P, M),
        "mask": a["mask_BxS2_bk0"],
        "ln1": a["L0_ffn_ln1_w"].reshape(DC, P).T,
        "ln2": a["L0_ffn_ln2_w"].reshape(DC, P).T,
        "wq": columns(a["L0_ffn_Wq"], HP),
        "wk": columns(a["L0_ffn_Wk"], HP),
        "wv": a["L0_ffn_Wv"],
        "wo": a["L0_ffn_Wo"],
        "a": a["L0_ffn_A"],
        "b": a["L0_ffn_B"].reshape(R, NF, P).transpose(1, 0, 2).reshape(NF, R * P),
        "w_in": columns(a["L0_ffn_W_in_base"], NF),
        "w_up": columns(a["L0_ffn_W_up_base"], NF),
        "w_down": a["L0_ffn_W_down"].T.reshape(NF, P, D),
    }
    laid = {k: np.ascontiguousarray(v) for k, v in laid.items()}
    nc = bacc.Bacc("TRN2", target_bir_lowering=False, num_devices=1)
    dram = {k: nc.dram_tensor("in_" + k, v.shape, mybir.dt.from_np(v.dtype), kind="ExternalInput").ap() for k, v in laid.items()}
    dram["out"] = nc.dram_tensor("out", (T, D), F32, kind="ExternalOutput").ap()
    program(nc, dram)
    r = run_bass_kernel_spmd(nc, [{"in_" + k: v for k, v in laid.items()}], core_ids=[0])
    return r.results[0]["out"].reshape(B, S, D)
```
